# Optimizing a Trainium2 kernel written in Bass

```python
import numpy as np
import jax
import jax.numpy as jnp

def _softmax(x, axis=-1):
    return jax.nn.softmax(x, axis=axis)

def _gelu(x):
    return jax.nn.gelu(x, approximate=True)

def _silu(x):
    return jax.nn.silu(x)

def _sigmoid(x):
    return jax.nn.sigmoid(x)

def _layernorm(x, axis=-1, eps=1e-05):
    m = jnp.mean(x, axis=axis, keepdims=True)
    v = jnp.var(x, axis=axis, keepdims=True)
    return (x - m) / jnp.sqrt(v + eps)

def _scatter_add(tgt, idx, src, axis=0):
    return tgt.at[idx].add(src)

def _segment_sum(src, seg, n):
    return jax.ops.segment_sum(src, seg, n)
kernel_name = 'mk_vit_tower_cls_d1_tok_img2048_r4_cd61d4'

def setup_inputs(seed: int=0):
    np.random.seed(seed)
    _w = jnp.asarray

    def _rec_inputs():
        import jax
        import jax.numpy as jnp
        _rk = jax.random.key(seed)
        x = -0.00340659 + 1.00146 * jax.random.normal(jax.random.fold_in(_rk, 1), (16, 256, 64, 2), jnp.float32)
        cls_tok = 0.02 * jax.random.normal(jax.random.fold_in(_rk, 5), (1, 1, 512), jnp.float32)
        return (x, cls_tok)
    x, cls_tok = _rec_inputs()

    def _L0_tok_setup():
        import jax, jax.numpy as jnp
        import numpy as np
        CH, H, N, N_SSM, SEQ_L = (1, 256, 64, 256, 512)

        def _kernel(C_ri, log_dt, B_ri, inv_A_real, A_imag, L):
            C = C_ri[..., 0] + 1j * C_ri[..., 1]
            B = B_ri[..., 0] + 1j * B_ri[..., 1]
            A = -jnp.exp(inv_A_real) + 1j * A_imag
            rep = log_dt.shape[0] // inv_A_real.shape[0]
            B = jnp.tile(B, (rep, 1))
            A = jnp.tile(A, (rep, 1))
            dt = jnp.exp(log_dt)
            dtA = A * dt[:, None]
            Ct = B[None] * C / (1.0 - dtA / 2) * dt[:, None]
            dA = (1.0 + dtA / 2) / (1.0 - dtA / 2)
            dA_log = jnp.log(dA)
            l = jnp.arange(L, dtype=jnp.float32)
            V = jnp.exp(dA_log[:, :, None] * l)
            K = 2.0 * jnp.einsum('chn,hnl->chl', Ct, V).real
            return K
        key = jax.random.key(seed)
        ks = jax.random.split(key, 5)
        return {'C_ri': jax.random.normal(ks[0], (CH, H, N, 2), dtype=jnp.float32), 'log_dt': jax.random.normal(ks[1], (H,), dtype=jnp.float32), 'B_ri': jax.random.normal(ks[2], (N_SSM, N, 2), dtype=jnp.float32), 'inv_A_real': jax.random.normal(ks[3], (N_SSM, N), dtype=jnp.float32), 'A_imag': jax.random.normal(ks[4], (N_SSM, N), dtype=jnp.float32), 'L': SEQ_L}
    _L0_tok_all = _L0_tok_setup()
    _L0_tok_in = {k: v for k, v in _L0_tok_all.items() if k in ('log_dt', 'B_ri', 'inv_A_real', 'A_imag')}
    del _L0_tok_all

    def _L0_attn_setup():
        import jax, jax.numpy as jnp
        import numpy as np
        B, T, D, S = (8, 1024, 512, 128)

        def _layernorm(x, gamma, beta, eps=1e-05):
            mu = jnp.mean(x, axis=-1, keepdims=True)
            var = jnp.var(x, axis=-1, keepdims=True)
            return (x - mu) * jax.lax.rsqrt(var + eps) * gamma + beta
        key = jax.random.key(seed)
        ks = jax.random.split(key, 9)
        sd = 0.02
        return {'x': jax.random.normal(ks[0], (B, T, D), dtype=jnp.float32), 'gamma': jnp.ones((D,), dtype=jnp.float32), 'beta': jnp.zeros((D,), dtype=jnp.float32), 'W_in': jax.random.normal(ks[1], (D, 3 * S), dtype=jnp.float32) * sd, 'b_in': jnp.zeros((3 * S,), dtype=jnp.float32), 'W_out': jax.random.normal(ks[2], (S, D), dtype=jnp.float32) * sd, 'b_out': jnp.zeros((D,), dtype=jnp.float32), 'W_skip': jax.random.normal(ks[3], (D, D), dtype=jnp.float32) * sd, 'b_skip': jnp.zeros((D,), dtype=jnp.float32)}
    _L0_attn_all = _L0_attn_setup()
    _L0_attn_in = {k: v for k, v in _L0_attn_all.items() if k in ('gamma', 'beta', 'W_in', 'b_in', 'W_out', 'b_out', 'W_skip', 'b_skip')}
    del _L0_attn_all

    def _L0_ffn_setup():
        import jax, jax.numpy as jnp
        import numpy as np
        B, S, D = (4, 128, 512)
        E, K, H = (8, 2, 352)
        HS = 2 * 352
        ALPHA = 0.001
        W_SCALE = 0.02

        def _moe_forward(hidden_states, gate_w, w_gate, w_up, w_down, sw_gate, sw_up, sw_down):
            b, s, d = hidden_states.shape
            x = hidden_states.reshape(-1, d)
            T = x.shape[0]
            logits = x @ gate_w
            scores = jax.nn.softmax(logits, axis=-1)
            topk_w, topk_idx = jax.lax.top_k(scores, K)
            mask = jax.nn.one_hot(topk_idx, E, dtype=scores.dtype).sum(axis=1)
            ce = mask.mean(axis=0)
            Pi = scores.mean(axis=0)
            aux_loss = (Pi * ce * E).sum() * ALPHA
            comb = jnp.zeros((T, E), dtype=x.dtype)
            comb = comb.at[jnp.arange(T)[:, None], topk_idx].add(topk_w)
            g = jax.nn.silu(jnp.einsum('td,edh->teh', x, w_gate)) * jnp.einsum('td,edh->teh', x, w_up)
            routed = jnp.einsum('teh,ehd,te->td', g, w_down, comb)
            shared = jax.nn.silu(x @ sw_gate) * (x @ sw_up) @ sw_down
            out = (routed + shared).reshape(b, s, d)
            return (out, aux_loss)
        key = jax.random.key(seed)
        ks = jax.random.split(key, 8)
        rn = lambda k, sh: jax.random.normal(k, sh, dtype=jnp.float32)
        return {'hidden_states': rn(ks[0], (B, S, D)), 'gate_w': rn(ks[1], (D, E)) * W_SCALE, 'w_gate': rn(ks[2], (E, D, H)) * W_SCALE, 'w_up': rn(ks[3], (E, D, H)) * W_SCALE, 'w_down': rn(ks[4], (E, H, D)) * W_SCALE, 'sw_gate': rn(ks[5], (D, HS)) * W_SCALE, 'sw_up': rn(ks[6], (D, HS)) * W_SCALE, 'sw_down': rn(ks[7], (HS, D)) * W_SCALE}
    _L0_ffn_all = _L0_ffn_setup()
    _L0_ffn_in = {k: v for k, v in _L0_ffn_all.items() if k in ('gate_w', 'w_gate', 'w_up', 'w_down', 'sw_gate', 'sw_up', 'sw_down')}
    del _L0_ffn_all
    return {'x': x, 'cls_tok': cls_tok, 'L0_tok_log_dt': _L0_tok_in['log_dt'], 'L0_tok_B_ri': _L0_tok_in['B_ri'], 'L0_tok_inv_A_real': _L0_tok_in['inv_A_real'], 'L0_tok_A_imag': _L0_tok_in['A_imag'], 'L0_attn_gamma': _L0_attn_in['gamma'], 'L0_attn_beta': _L0_attn_in['beta'], 'L0_attn_W_in': _L0_attn_in['W_in'], 'L0_attn_b_in': _L0_attn_in['b_in'], 'L0_attn_W_out': _L0_attn_in['W_out'], 'L0_attn_b_out': _L0_attn_in['b_out'], 'L0_attn_W_skip': _L0_attn_in['W_skip'], 'L0_attn_b_skip': _L0_attn_in['b_skip'], 'L0_ffn_gate_w': _L0_ffn_in['gate_w'], 'L0_ffn_w_gate': _L0_ffn_in['w_gate'], 'L0_ffn_w_up': _L0_ffn_in['w_up'], 'L0_ffn_w_down': _L0_ffn_in['w_down'], 'L0_ffn_sw_gate': _L0_ffn_in['sw_gate'], 'L0_ffn_sw_up': _L0_ffn_in['sw_up'], 'L0_ffn_sw_down': _L0_ffn_in['sw_down']}

def reference(x, cls_tok, L0_tok_log_dt, L0_tok_B_ri, L0_tok_inv_A_real, L0_tok_A_imag, L0_attn_gamma, L0_attn_beta, L0_attn_W_in, L0_attn_b_in, L0_attn_W_out, L0_attn_b_out, L0_attn_W_skip, L0_attn_b_skip, L0_ffn_gate_w, L0_ffn_w_gate, L0_ffn_w_up, L0_ffn_w_down, L0_ffn_sw_gate, L0_ffn_sw_up, L0_ffn_sw_down):
    import jax
    import jax.numpy as jnp

    def _L0_tok_ref(C_ri, log_dt, B_ri, inv_A_real, A_imag, L):
        import jax, jax.numpy as jnp
        import numpy as np
        CH, H, N, N_SSM, SEQ_L = (1, 256, 64, 256, 512)

        def _kernel(C_ri, log_dt, B_ri, inv_A_real, A_imag, L):
            C = C_ri[..., 0] + 1j * C_ri[..., 1]
            B = B_ri[..., 0] + 1j * B_ri[..., 1]
            A = -jnp.exp(inv_A_real) + 1j * A_imag
            rep = log_dt.shape[0] // inv_A_real.shape[0]
            B = jnp.tile(B, (rep, 1))
            A = jnp.tile(A, (rep, 1))
            dt = jnp.exp(log_dt)
            dtA = A * dt[:, None]
            Ct = B[None] * C / (1.0 - dtA / 2) * dt[:, None]
            dA = (1.0 + dtA / 2) / (1.0 - dtA / 2)
            dA_log = jnp.log(dA)
            l = jnp.arange(L, dtype=jnp.float32)
            V = jnp.exp(dA_log[:, :, None] * l)
            K = 2.0 * jnp.einsum('chn,hnl->chl', Ct, V).real
            return K
        return _kernel(C_ri, log_dt, B_ri, inv_A_real, A_imag, L)

    def _L0_attn_ref(x, gamma, beta, W_in, b_in, W_out, b_out, W_skip, b_skip):
        import jax, jax.numpy as jnp
        import numpy as np
        B, T, D, S = (8, 1024, 512, 128)

        def _layernorm(x, gamma, beta, eps=1e-05):
            mu = jnp.mean(x, axis=-1, keepdims=True)
            var = jnp.var(x, axis=-1, keepdims=True)
            return (x - mu) * jax.lax.rsqrt(var + eps) * gamma + beta
        u = _layernorm(x, gamma, beta)
        gates = jnp.einsum('btd,de->bte', u, W_in) + b_in
        S_ = W_out.shape[0]
        delta, b_proj, c_proj = (gates[..., :S_], gates[..., S_:2 * S_], gates[..., 2 * S_:])
        alpha = jax.nn.sigmoid(delta)
        tc = jnp.tanh(c_proj)

        def step(h, inp):
            a_t, b_t, tc_t = inp
            h = (1.0 - a_t) * h + a_t * b_t
            return (h, h * tc_t)
        h0 = jnp.zeros((x.shape[0], S_), dtype=x.dtype)
        _, y = jax.lax.scan(step, h0, (alpha.transpose(1, 0, 2), b_proj.transpose(1, 0, 2), tc.transpose(1, 0, 2)))
        y = y.transpose(1, 0, 2)
        out = jnp.einsum('bts,sd->btd', y, W_out) + b_out
        out = out + jnp.einsum('btd,de->bte', x, W_skip) + b_skip
        return out

    def _L0_ffn_ref(hidden_states, gate_w, w_gate, w_up, w_down, sw_gate, sw_up, sw_down):
        import jax, jax.numpy as jnp
        import numpy as np
        B, S, D = (4, 128, 512)
        E, K, H = (8, 2, 352)
        HS = 2 * 352
        ALPHA = 0.001
        W_SCALE = 0.02

        def _moe_forward(hidden_states, gate_w, w_gate, w_up, w_down, sw_gate, sw_up, sw_down):
            b, s, d = hidden_states.shape
            x = hidden_states.reshape(-1, d)
            T = x.shape[0]
            logits = x @ gate_w
            scores = jax.nn.softmax(logits, axis=-1)
            topk_w, topk_idx = jax.lax.top_k(scores, K)
            mask = jax.nn.one_hot(topk_idx, E, dtype=scores.dtype).sum(axis=1)
            ce = mask.mean(axis=0)
            Pi = scores.mean(axis=0)
            aux_loss = (Pi * ce * E).sum() * ALPHA
            comb = jnp.zeros((T, E), dtype=x.dtype)
            comb = comb.at[jnp.arange(T)[:, None], topk_idx].add(topk_w)
            g = jax.nn.silu(jnp.einsum('td,edh->teh', x, w_gate)) * jnp.einsum('td,edh->teh', x, w_up)
            routed = jnp.einsum('teh,ehd,te->td', g, w_down, comb)
            shared = jax.nn.silu(x @ sw_gate) * (x @ sw_up) @ sw_down
            out = (routed + shared).reshape(b, s, d)
            return (out, aux_loss)
        out, _aux = _moe_forward(hidden_states, gate_w, w_gate, w_up, w_down, sw_gate, sw_up, sw_down)
        return out
    h = _L0_tok_ref(x, L0_tok_log_dt, L0_tok_B_ri, L0_tok_inv_A_real, L0_tok_A_imag, 512)
    h = jnp.concatenate([jnp.broadcast_to(cls_tok, (h.shape[0], 1, h.shape[2])), h], axis=1)
    h = h + _L0_attn_ref(_layernorm(h, axis=-1), L0_attn_gamma, L0_attn_beta, L0_attn_W_in, L0_attn_b_in, L0_attn_W_out, L0_attn_b_out, L0_attn_W_skip, L0_attn_b_skip)
    h = h + _L0_ffn_ref(_layernorm(h, axis=-1), L0_ffn_gate_w, L0_ffn_w_gate, L0_ffn_w_up, L0_ffn_w_down, L0_ffn_sw_gate, L0_ffn_sw_up, L0_ffn_sw_down)
    return h

_drawn_inputs = setup_inputs


def setup_inputs(seed=0):
    import zlib

    import numpy as np

    out = dict(_drawn_inputs(seed))
    spreads = {'L0_attn_gamma': (1.0, 0.6),
     'L0_attn_beta': (0.0, 0.8),
     'L0_attn_b_in': (0.0, 0.8),
     'L0_attn_b_out': (0.0, 0.1),
     'L0_attn_b_skip': (0.0, 0.1)}
    factors = {'L0_ffn_gate_w': 6.678,
     'L0_ffn_w_gate': 6.11,
     'L0_ffn_w_up': 5.955,
     'L0_ffn_w_down': 5.973,
     'L0_ffn_sw_gate': 8.0,
     'L0_ffn_sw_up': 8.0,
     'L0_ffn_sw_down': 8.0}
    for name, (base, spread) in spreads.items():
        noise = np.random.default_rng([zlib.crc32(name.encode()), seed]).standard_normal(out[name].shape)
        drawn = base * np.exp(spread * noise) if base else spread * noise
        out[name] = jnp.asarray(drawn.astype(out[name].dtype))
    for name, factor in factors.items():
        out[name] = (out[name] * factor).astype(out[name].dtype)
    return out
```

```python
import concourse.bass as bass
from concourse import mybir
from contextlib import ExitStack

F32 = mybir.dt.float32
F16 = mybir.dt.float16
I32 = mybir.dt.int32
ALU = mybir.AluOpType
ACT = mybir.ActivationFunctionType
AX = mybir.AxisListType

P = 128
B, T, N, D = 16, 256, 64, 512
S = 128
E, H = 8, 352
HS = 2 * H
EPS = 1e-5
KD = D // P
J = T // 2
NB = 8
NA = D // NB
TC = 16
JC = TC // 2
NCH = T // TC
TOK = B * TC
TILES = 1 + 2 * NCH
SHM = 5
SHT = HS - SHM * P
KH = (H + P - 1) // P
HK = [min(P, H - i * P) for i in range(KH)]
SW, SX, SY = 64.0, 256.0, 4.0
SXW = 1.0 / (SX * SW)
CAP = ((B * T + 1 + P - 1) // P + 1) * P
NSLOT = (2 * (B * T + 1) + E * (P - 1)) // P + 1
NSLOT += NSLOT % 2
ZERO = E * CAP
DUMP = ZERO + P
NR = DUMP + 2 * P
UG = (KD // 2) * 2 * 2 * H
UD = KH * 2 * (D // 2)
UW = UG + UD
NBUF = 4
PER_POOL, PER_DVE = 11, 52


def at_least(eng, sem, value):
    if isinstance(value, int) and value <= 0:
        return
    eng.wait_ge(sem, value)


def apart(eng, sem):
    eng.sem_inc(sem, 1)


class Chain:

    def __init__(self, eng, sem):
        self.eng, self.sem, self.n = eng, sem, 0
        self.loop = None

    def value(self):
        if self.loop is None:
            return self.n
        i, first, start, per = self.loop
        return (i - first) * per + self.n

    def do(self, ins):
        ins.then_inc(self.sem, 1)
        self.n += 1

    def sync(self):
        self.eng.wait_ge(self.sem, self.value())

    def link(self, ins):
        self.do(ins)
        self.sync()

    def enter(self, i, first, per):
        self.loop = (i, first, self.n, per)

    def leave(self, trips):
        i, first, start, per = self.loop
        assert self.n - start == per, ("instructions in the loop", self.n - start)
        self.n = start + per * trips
        self.loop = None


def vit_tower(nc, x, cls_tok, log_dt, b_ri, inv_a_real, a_imag, gamma, beta, w_in, b_in, w_out, b_out,
              w_skip, b_skip, gate_w, w_gate, w_up, w_down, sw_gate, sw_up, sw_down, out):
    top = ExitStack()

    def sem(name):
        return top.enter_context(nc.semaphore(name))

    def sb_in(stack):
        return lambda name, shape, dt: stack.enter_context(nc.sbuf_tensor(name, shape, dt))

    hs_d = nc.dram_tensor("h_tok", [NCH, TOK, D], F32).ap()
    xs_d = nc.dram_tensor("x_slots", [NR, 2 * D], F16).ap()
    ys_d = nc.dram_tensor("y_slots", [NSLOT * P, D], F32).ap()
    rs_d = nc.dram_tensor("resid", [TILES * P, D], F32).ap()
    w16_d = nc.dram_tensor("w_halves", [2 * E, P, UW], F16).ap()

    with top:
        keep = sb_in(top)
        psum = [top.enter_context(nc.psum_tensor(f"bank{i}", [P, D], F32)) for i in range(8)]

        slots = keep("slots", [P, TILES, 2], F32)
        rows_y = keep("rows_y", [P, TILES + NBUF, 2], I32)
        logits = keep("logits", [P, TILES, E], F32)
        top_l = keep("top_l", [P, TILES, 2], F32)
        run = keep("run", [P, E], F32)
        ident16 = keep("ident16", [P, P], F16)
        pcol = keep("pcol", [P, 1], F32)
        zrow = keep("zrow", [P, 2 * D], F16)
        rev = keep("rev", [P, 2, E], F32)

        phase1 = ExitStack()
        sb = sb_in(phase1)
        wsgu = sb("wsgu", [P, KD, 2, 2 * HS], F16)
        wsd = sb("wsd", [P, SHM + 1, 2, D], F16)
        win = sb("win", [P, KD, 2, 3 * S], F16)
        wout = sb("wout", [P, 2, D], F16)
        wskip = sb("wskip", [P, KD, 2, D], F16)
        gw = sb("gw", [P, KD, 2, E], F16)
        brow = sb("brow", [1, 2, D], F16)
        ones_row = sb("ones_row", [1, P], F16)
        tri = sb("tri", [P, P], F16)
        ones16 = sb("ones16", [P, P], F16)
        cb = sb("cb", [P, 3], F32)
        cbh = sb("cbh", [P, 1], F32)
        mask0 = sb("mask0", [P, 1], F32)
        dump_s = sb("dump_s", [P, 2], F32)
        cT = sb("cT", [P, 2, B, J], F32)
        pe_ = sb("pe", [P, 2, NB, J], F32)
        pg = sb("pg", [P, 2, NB, J], F32)
        ph = sb("ph", [P, 2, NB, J], F32)

        with ExitStack() as ph0:
            t0 = sb_in(ph0)
            xj = t0("xj", [P, B, 2 * N, 2], F32)
            cj = t0("cj", [P, 2, B, 2 * N], F32)
            ctmp = t0("ctmp", [P, 2, B, 2 * N], F32)
            bj = t0("bj", [P, 2 * N, 2], F32)
            aj = t0("aj", [P, 2, 2 * N], F32)
            dtj = t0("dtj", [P, 2], F32)
            pw_ = t0("pw_", [P, 24, 2 * N], F32)
            dj = t0("dj", [P, 2, 2 * N], F32)
            mtmp = t0("mtmp", [P, 2, 2, 4 * J], F32)
            sq = t0("sq", [P, 4, 2, J], F32)
            identf = t0("identf", [P, P], F32)
            gam = t0("gam", [P, KD], F32)
            bet = t0("bet", [P, KD], F32)
            bin_ = t0("bin_", [P, 3], F32)
            bo = t0("bo", [1, 3, D], F32)
            st = [t0(f"st{i}", [P, 4, D], F32) for i in range(2)]
            io = t0("io", [P, 2, E], I32)
            pi = t0("pi", [P, 1], I32)

            p_in = sem("p_in")
            p_x = sem("p_x")
            st_in = [sem("st_in0"), sem("st_in1")]
            st_hi = sem("st_hi")
            st_lo = sem("st_lo")
            p_act = sem("p_act")
            p_gp = sem("p_gp")
            p_v = sem("p_v")
            p_ct = sem("p_ct")
            p_tp = sem("p_tp")
            p_te = sem("p_te")
            p_cb = sem("p_cb")
            p_z = sem("p_z")
            p_bw = sem("p_bw")

            def rows(w):
                return w.rearrange("(k p) n -> p k n", p=P)

            jobs = [("win", rows(w_in), 3 * S)]
            jobs += [("wskip", rows(w_skip), D)]
            jobs += [("wout", w_out.rearrange("(k p) n -> p k n", p=P), D)]
            jobs += [("gw", rows(gate_w), E)]
            for kind, w in (("g", sw_gate), ("u", sw_up)):
                r = rows(w)
                jobs += [(kind + "0", r[:, :, 0:SHM * P // 2], SHM * P // 2), (kind + "1", r[:, :, SHM * P // 2:SHM * P], SHM * P // 2),
                         (kind + "t", r[:, :, SHM * P:HS], SHT)]
            jobs += [("d0", sw_down[0:4 * P, :].rearrange("(k p) n -> p k n", p=P), D)]
            jobs += [("d1", sw_down[4 * P:5 * P, :].rearrange("(k p) n -> p k n", p=P), D)]
            jobs += [("d2", sw_down[5 * P:HS, :].rearrange("(k p) n -> p k n", k=1), D)]

            def half(kind, h):
                if kind == "win":
                    return win[:, :, h, :]
                if kind == "wskip":
                    return wskip[:, :, h, :]
                if kind == "wout":
                    return wout[:, h:h + 1, :]
                if kind == "gw":
                    return gw[:, :, h, :]
                if kind == "d0":
                    return wsd[:, 0:4, h, :]
                if kind == "d1":
                    return wsd[:, 4:5, h, :]
                if kind == "d2":
                    return wsd[SHT:2 * SHT, 5:6, h, :]
                c0 = 0 if kind[0] == "g" else SHM * P
                if kind[1] == "t":
                    c0, n = 2 * SHM * P + (0 if kind[0] == "g" else SHT), SHT
                else:
                    n = SHM * P // 2
                    c0 += int(kind[1]) * n
                return wsgu[:, :, h, c0:c0 + n]

            def staged(i):
                kind, src, n = jobs[i]
                k = src.shape[1]
                if kind == "d2":
                    return st[i % 2][SHT:2 * SHT, 0:1, 0:n]
                return st[i % 2][:, 0:k, 0:n]

            block = ph0.enter_context(nc.Block())

            @block.sync
            def _(sp):
                sp.dma_start(dtj[:], log_dt.rearrange("(j t) -> j t", t=2)).then_inc(p_in, 16)
                sp.dma_start(aj[:, 0, :], inv_a_real.rearrange("(j t) n -> j (t n)", t=2)).then_inc(p_in, 16)
                sp.dma_start(aj[:, 1, :], a_imag.rearrange("(j t) n -> j (t n)", t=2)).then_inc(p_in, 16)
                sp.dma_start(bj[:], b_ri.rearrange("(j t) n r -> j (t n) r", t=2)).then_inc(p_in, 16)
                sp.dma_start(gam[:], gamma.rearrange("(k p) -> p k", p=P), allow_slow_non_contiguous=True).then_inc(p_in, 16)
                sp.dma_start(bet[:], beta.rearrange("(k p) -> p k", p=P), allow_slow_non_contiguous=True).then_inc(p_in, 16)
                sp.dma_start(bin_[:], b_in.rearrange("(k p) -> p k", p=P), allow_slow_non_contiguous=True).then_inc(p_in, 16)
                sp.dma_start(bo[:, 0, :], b_out.rearrange("(a n) -> a n", a=1)).then_inc(p_in, 16)
                sp.dma_start(bo[:, 1, :], b_skip.rearrange("(a n) -> a n", a=1)).then_inc(p_in, 16)
                sp.dma_start(xj[:].rearrange("j c n r -> j c (n r)"),
                             x.rearrange("c (j t) n r -> j c (t n r)", t=2)).then_inc(p_x, 16)
                for i, (kind, src, n) in enumerate(jobs):
                    at_least(sp, st_lo, i - 1)
                    if i == 2:
                        sp.wait_ge(p_cb, 1)
                    sp.dma_start(staged(i), src).then_inc(st_in[i % 2], 16)
                sp.wait_ge(p_gp, 5)
                sp.dma_start(xs_d[ZERO:ZERO + P, :], zrow[:]).then_inc(p_z, 16)
                sp.wait_ge(p_z, 16)

            @block.gpsimd
            def _(gp):
                nc.gpsimd.memset(ident16[:], 0.0).then_inc(p_gp, 1)
                nc.gpsimd.memset(identf[:], 0.0).then_inc(p_gp, 1)
                nc.gpsimd.memset(tri[:], 1.0).then_inc(p_gp, 1)
                nc.gpsimd.memset(ones16[:], 1.0).then_inc(p_gp, 1)
                nc.gpsimd.memset(zrow[:], 0.0).then_inc(p_gp, 1)
                nc.gpsimd.memset(ones_row[:], 1.0).then_inc(p_gp, 1)
                gp.wait_ge(p_gp, 6)
                for m in (ident16, identf):
                    nc.gpsimd.affine_select(out=m[:], in_=m[:], compare_op=ALU.not_equal, fill=1.0, base=0,
                                            pattern=[[-1, P]], channel_multiplier=1).then_inc(p_gp, 1)
                nc.gpsimd.affine_select(out=tri[:], in_=tri[:], compare_op=ALU.is_gt, fill=0.0, base=0,
                                        pattern=[[1, P]], channel_multiplier=-1).then_inc(p_gp, 1)
                nc.gpsimd.iota(io[:], pattern=[[0, 2], [1, E]], base=0, channel_multiplier=0).then_inc(p_gp, 1)
                nc.gpsimd.iota(pi[:], pattern=[[0, 1]], base=0, channel_multiplier=1).then_inc(p_gp, 1)

            @block.scalar
            def _(act):
                act.wait_ge(p_in, 9 * 16)
                nc.scalar.activation(pw_[:, 0, 0:2], dtj[:], ACT.Exp).then_inc(p_act, 1)
                nc.scalar.activation(pw_[:, 1, :], aj[:, 0, :], ACT.Exp).then_inc(p_act, 1)
                for i, (kind, src, n) in enumerate(jobs):
                    act.wait_ge(st_in[i % 2], 16 * (i // 2 + 1))
                    if kind == "win":
                        act.wait_ge(p_bw, 1)
                    nc.scalar.activation(half(kind, 0), staged(i), ACT.Copy, scale=SW).then_inc(st_hi, 1)

            @block.tensor
            def _(pe):
                pe.wait_ge(p_gp, 8)
                pe.wait_ge(st_in[0], 16)
                pe.wait_ge(p_in, 9 * 16)
                for m in range(3):
                    for k in range(KD):
                        last = nc.tensor.matmul(psum[7][:, m:m + 1], st[0][:, k, m * S:(m + 1) * S],
                                                bet[:, k:k + 1], start=(k == 0), stop=(k == KD - 1))
                last.then_inc(p_cb, 1)
                pe.wait_ge(p_ct, 1)
                for r in range(2):
                    last = nc.tensor.transpose(psum[0][:, r * J:(r + 1) * J], dj[:, r, :], identf[:])
                last.then_inc(p_tp, 1)
                pe.wait_ge(p_ct, 2)
                for g in range(8):
                    r, c0 = g // 4, (g % 4) * 4
                    if g >= 1:
                        at_least(pe, p_te, g)
                    for c in range(4):
                        last = nc.tensor.transpose(psum[1 + g % 2][:, c * J:(c + 1) * J],
                                                   cj[:, r, c0 + c, :], identf[:])
                    last.then_inc(p_tp, 1)

            @block.vector
            def _(v):
                ch = Chain(v, p_v)
                link = ch.link
                TT, TS, STT = nc.vector.tensor_tensor, nc.vector.tensor_scalar, nc.vector.scalar_tensor_tensor
                v.wait_ge(p_in, 9 * 16)
                v.wait_ge(p_act, 2)
                w = lambda i: pw_[:, i, :]
                dtb = pw_[:, 0, 0:2].rearrange("p (t o) -> p t o", o=1).broadcast_to([P, 2, N])
                two = lambda ap: ap.rearrange("p (t n) -> p t n", t=2)
                link(TT(two(w(2)), two(w(1)), dtb, ALU.mult))
                link(TS(w(2), w(2), -0.5, None, ALU.mult))
                link(TT(two(w(3)), two(aj[:, 1, :]), dtb, ALU.mult))
                link(TS(w(3), w(3), 0.5, None, ALU.mult))
                link(TS(w(4), w(2), -1.0, 1.0, ALU.mult, ALU.add))
                link(TT(w(5), w(4), w(4), ALU.mult))
                link(TT(w(6), w(3), w(3), ALU.mult))
                link(TT(w(7), w(5), w(6), ALU.add))
                link(nc.vector.reciprocal(w(8), w(7)))
                link(TS(w(9), w(2), 1.0, None, ALU.add))
                link(TT(w(10), w(9), w(4), ALU.mult))
                link(TT(w(10), w(10), w(6), ALU.subtract))
                link(TT(dj[:, 0, :], w(10), w(8), ALU.mult))
                link(TS(w(11), w(3), 2.0, None, ALU.mult))
                v.wait_ge(p_gp, 11)
                TT(dj[:, 1, :], w(11), w(8), ALU.mult).then_inc(p_ct, 1)
                br, bi = bj[:, :, 0], bj[:, :, 1]
                link(TT(w(12), br, w(4), ALU.mult))
                link(TT(w(13), bi, w(3), ALU.mult))
                link(TT(w(12), w(12), w(13), ALU.subtract))
                link(TT(w(14), br, w(3), ALU.mult))
                link(TT(w(15), bi, w(4), ALU.mult))
                link(TT(w(14), w(14), w(15), ALU.add))
                link(TT(two(w(16)), two(w(8)), dtb, ALU.mult))
                link(TS(w(16), w(16), 2.0, None, ALU.mult))
                link(TT(w(12), w(12), w(16), ALU.mult))
                link(TT(w(14), w(14), w(16), ALU.mult))
                v.wait_ge(p_x, 16)
                xr, xi = xj[:, :, :, 0], xj[:, :, :, 1]
                fr = pw_[:, 12:13, :].broadcast_to([P, B, 2 * N])
                fi = pw_[:, 14:15, :].broadcast_to([P, B, 2 * N])
                ch.do(TT(ctmp[:, 0], xr, fr, ALU.mult))
                link(TT(ctmp[:, 1], xi, fi, ALU.mult))
                link(TT(cj[:, 0], ctmp[:, 0], ctmp[:, 1], ALU.subtract))
                ch.do(TT(ctmp[:, 0], xr, fi, ALU.mult))
                link(TT(ctmp[:, 1], xi, fr, ALU.mult))
                TT(cj[:, 1], ctmp[:, 0], ctmp[:, 1], ALU.add).then_inc(p_ct, 1)
                link(TS(rev[:], io[:], -1.0, float(E), ALU.mult, ALU.add))
                link(nc.vector.tensor_copy(pcol[:], pi[:]))
                link(TS(mask0[:], pcol[:], 0.0, None, ALU.is_equal))
                link(TS(run[:], io[:, 0, :], float(CAP), None, ALU.mult))
                link(TS(dump_s[:, 0:1], mask0[:], -1.0, 1.0, ALU.mult, ALU.add))
                link(TS(dump_s[:, 1:2], pcol[:], float(DUMP + P), dump_s[:, 0:1], ALU.add, ALU.mult))
                link(TS(dump_s[:, 0:1], pcol[:], float(DUMP), dump_s[:, 0:1], ALU.add, ALU.mult))
                v.wait_ge(p_cb, 1)
                link(TT(cb[:], psum[7][:, 0:3], bin_[:], ALU.add))
                link(TS(cbh[:], cb[:, 0:1], 0.5, None, ALU.mult))
                link(TT(bo[:, 2, :], bo[:, 0, :], bo[:, 1, :], ALU.add))
                link(TS(brow[:, 0, :], bo[:, 2, :], SW * SY, None, ALU.mult))
                link(STT(brow[:, 1, :], bo[:, 2, :], SW * SY, brow[:, 0, :], ALU.mult, ALU.subtract))
                for k in range(KD):
                    last = TS(st[0][:, k, 0:3 * S], st[0][:, k, 0:3 * S], gam[:, k:k + 1], None, ALU.mult)
                last.then_inc(p_bw, 1)
                link(nc.vector.memset(rows_y[:, TILES:, :], 0))
                link(nc.vector.memset(pe_[:, 0, 0:1, :], 1.0))
                for tab in (pe_, pg, ph):
                    if tab is not pe_:
                        link(nc.vector.memset(tab[:, 0, 0:1, :], 1.0))
                    link(nc.vector.memset(tab[:, 1, 0:1, :], 0.0))
                v.wait_ge(p_tp, 1)
                for r in range(2):
                    link(nc.vector.tensor_copy(pe_[:, r, 1, :], psum[0][:, r * J:(r + 1) * J]))

                def cmul(dst, a, b, n):
                    m = lambda i: mtmp[:, i].rearrange("p r (n j) -> p r n j", j=J)[:, :, 0:n, :]
                    for r in range(2):
                        w = b[:, r:r + 1].rearrange("p r (o j) -> p r o j", o=1).broadcast_to([P, 2, n, J])
                        (ch.do if r == 0 else link)(TT(m(r), a, w, ALU.mult))
                    ch.do(TT(dst[:, 0], m(0)[:, 0], m(1)[:, 1], ALU.subtract))
                    link(TT(dst[:, 1], m(0)[:, 1], m(1)[:, 0], ALU.add))

                for n, tab in enumerate((pe_, pg, ph)):
                    cmul(sq[:, 0, :, :].rearrange("p r (o j) -> p r o j", o=1), tab[:, 0:2, 1:2, :], tab[:, 0:2, 1, :], 1)
                    cmul(tab[:, 0:2, 2:4, :], tab[:, 0:2, 0:2, :], sq[:, 0], 2)
                    cmul(sq[:, 1, :, :].rearrange("p r (o j) -> p r o j", o=1), sq[:, 0].rearrange("p r (o j) -> p r o j", o=1), sq[:, 0], 1)
                    cmul(tab[:, 0:2, 4:8, :], tab[:, 0:2, 0:4, :], sq[:, 1], 4)
                    if n < 2:
                        cmul((pg, ph)[n][:, 0:2, 1:2, :], sq[:, 1].rearrange("p r (o j) -> p r o j", o=1), sq[:, 1], 1)
                for g in range(8):
                    r, c0 = g // 4, (g % 4) * 4
                    v.wait_ge(p_tp, g + 2)
                    nc.vector.tensor_copy(cT[:, r, c0:c0 + 4, :].rearrange("p c j -> p (c j)"),
                                          psum[1 + g % 2][:]).then_inc(p_te, 1)
                for i, (kind, src, n) in enumerate(jobs):
                    v.wait_ge(st_hi, i + 1)
                    k = src.shape[1]
                    for c in range(k):
                        last = STT(half(kind, 1)[:, c, :], staged(i)[:, c, :], SW, half(kind, 0)[:, c, :],
                                   ALU.mult, ALU.subtract)
                    last.then_inc(st_lo, 1)

        hx = sb("hx", [P, 2, D], F32)
        hc = sb("hc", [P, 2, D], F32)
        xf = sb("xf", [P, 2, D], F32)
        x2r = sb("x2r", [P, 2, 2, D], F16)
        x2T = sb("x2T", [P, 2, KD, TOK], F16)
        x3r = sb("x3r", [P, 2, 2, D], F16)
        x3T = sb("x3T", [P, 2, KD, TOK], F16)
        h2 = sb("h2", [P, 2, D], F32)
        r_o = sb("r_o", [P, 2, D], F32)
        stat = sb("stat", [P, 2, 2, 6], F32)
        mv = sb("mv", [P, 2, 2, 2], F32)
        sc = sb("sc", [P, 8, 2], F32)
        pwc = sb("pwc", [P, 2, 2], F32)
        ir = sb("ir", [P, 2], F32)
        th = sb("th", [P, TOK], F32)
        tc = sb("tc", [P, TOK], F32)
        al = sb("al", [P, TOK], F32)
        om = sb("om", [P, TOK], F32)
        bb = sb("bb", [P, TOK], F32)
        hsc = sb("hsc", [P, TOK], F32)
        carry = sb("carry", [P, B], F32)
        fix = sb("fix", [P, B], F32)
        yT = sb("yT", [P, 2, TOK], F16)
        sgs = sb("sgs", [P, 2, TOK], F32)
        gf = sb("gf", [P, 2, TOK], F32)
        gT = sb("gT", [P, SHM + 1, 2, TOK], F16)
        ea = sb("ea", [P, 2, JC, 2, NA], F32)
        et = sb("et", [P, 4, JC, NA], F32)
        pp = sb("pp", [P, 2, JC, NB, B], F32)
        pt = sb("pt", [P, 2, JC, NB, B], F32)
        hst = sb("hst", [P, JC, 2, NA], F32)
        rt = sb("rt", [P, 8, 2, E], F32)
        rm = sb("rm", [P, 8, 2], F32)
        m16 = sb("m16", [P, 2, E], F16)
        oh = sb("oh", [P, 2, 2, E], F32)
        zi = sb("zi", [P, E], I32)
        sl = sb("sl", [P, 2, 2], I32)

        HK2 = KD // 2
        rgu = sb("rgu", [P, 2, HK2, H], F32)
        rdn = sb("rdn", [P, KH, D // 2], F32)
        hgu = sb("hgu", [P, HK2, 2, 2 * H], F16)
        hdn = sb("hdn", [P, KH, 2, D // 2], F16)

        BX = [psum[0], psum[3]]
        BU = [psum[1], psum[2]]
        BD, BS, BY, BG, BB = psum[3], psum[4], psum[5], psum[6], psum[7]

        c_tokp = sem("c_tokp")
        c_tokm = sem("c_tokm")
        c_toke = sem("c_toke")
        c_hst = sem("c_hst")
        c_hx = sem("c_hx")
        c_prom = sem("c_prom")
        c_irc = sem("c_irc")
        c_st2 = sem("c_st2")
        c_pw2 = sem("c_pw2")
        c_xf2 = sem("c_xf2")
        c_hi2 = sem("c_hi2")
        c_lo2 = sem("c_lo2")
        c_t2 = sem("c_t2")
        c_e2 = sem("c_e2")
        c_gt = sem("c_gt")
        c_th = sem("c_th")
        c_yf = sem("c_yf")
        c_yh = sem("c_yh")
        c_yl = sem("c_yl")
        c_out = sem("c_out")
        c_oev = sem("c_oev")
        c_st3 = sem("c_st3")
        c_pw3 = sem("c_pw3")
        c_xf3 = sem("c_xf3")
        c_hi3 = sem("c_hi3")
        c_lo3 = sem("c_lo3")
        c_t3 = sem("c_t3")
        c_e3 = sem("c_e3")
        c_rt = sem("c_rt")
        c_m = sem("c_m")
        c_rk = sem("c_rk")
        c_sl = sem("c_sl")
        c_sca = sem("c_sca")
        c_up = sem("c_up")
        c_sg = sem("c_sg")
        c_gm = sem("c_gm")
        c_gh = sem("c_gh")
        c_gl = sem("c_gl")
        c_dn = sem("c_dn")
        c_dev = sem("c_dev")
        c_ro = sem("c_ro")
        c_sep = sem("c_sep")
        c_wi = sem("c_wi")
        c_wh = sem("c_wh")
        c_wl = sem("c_wl")
        c_wo = sem("c_wo")
        c_v = sem("c_v")
        c_p = sem("c_p")
        c_cst = sem("c_cst")

        tiles = lambda k: 1 if isinstance(k, int) and k == 0 else 2
        cols = lambda k: tiles(k) * P
        LOOP0, LOOP1 = 2, NCH - 1
        LAST = NCH + 1
        clampc = lambda k: k if not isinstance(k, int) else min(k, NCH)

        def iterate(eng, body, chain=None, per=None):
            body(-1)
            for k in range(LOOP0):
                body(k)
            with eng.Fori(LOOP0, LOOP1) as k:
                if chain is not None:
                    chain.enter(k, LOOP0, per)
                body(k)
            if chain is not None:
                chain.leave(LOOP1 - LOOP0)
            for k in range(LOOP1, LAST + 1):
                body(k)

        has = lambda k: not isinstance(k, int) or 0 <= k <= NCH
        htok = lambda k: not isinstance(k, int) or 1 <= k <= NCH
        rows_of = lambda k: (0 if isinstance(k, int) and k == 0 else k * 2 - 1)

        with nc.Block() as block:

            @block.sync
            def _(sp):
                w_g = w_gate.rearrange("e (s k p) n -> (e s) p k n", s=2, p=P)
                w_u = w_up.rearrange("e (s k p) n -> (e s) p k n", s=2, p=P)
                one = lambda ap, u: ap[bass.ds(u, 1)]

                def load_unit(u):
                    for g, w in enumerate((w_g, w_u)):
                        sp.dma_start(rgu[:, g], one(w, u).rearrange("u p k n -> (u p) k n")).then_inc(c_wi, 16)
                    e, c = u // 2, u % 2 * (D // 2)
                    src = w_down[bass.ds(e, 1), :, bass.ds(c, D // 2)].rearrange("e h d -> (e h) d")
                    sp.dma_start(rdn[:, 0:2, :], src[0:2 * P].rearrange("(k p) d -> p k d", p=P)).then_inc(c_wi, 16)
                    sp.dma_start(rdn[0:HK[2], 2, :], src[2 * P:H]).then_inc(c_wi, 16)

                def store_unit(u):
                    dst = one(w16_d, u).rearrange("u p n -> (u p) n")
                    sp.dma_start(dst[:, 0:UG], hgu[:].rearrange("p k h n -> p (k h n)")).then_inc(c_wo, 16)
                    sp.dma_start(dst[:, UG:UW], hdn[:].rearrange("p k h n -> p (k h n)")).then_inc(c_wo, 16)

                def body(k):
                    if htok(k - 1):
                        sp.wait_ge(c_wl, k - 1)
                        store_unit(k - 2)
                    if htok(k):
                        load_unit(k - 1)
                    if htok(k + 1):
                        n = k + 1
                        sp.wait_ge(c_hst, n * NB * 16)
                        at_least(sp, c_prom, n)
                        sp.wait_ge(c_lo2, n)
                        src = hs_d[bass.ds(n - 1, 1)].rearrange("q (i p) d -> p (q i) d", p=P)
                        sp.dma_start(hx[:], src).then_inc(c_hx, 16)
                    elif k + 1 == 0:
                        sp.dma_start(hx[:, 0, :], cls_tok.rearrange("a b d -> (a b) d").broadcast_to([P, D])).then_inc(c_hx, 16)
                    if htok(k + 2):
                        n = k + 2
                        sp.wait_ge(c_toke, n * 2)
                        dst = hs_d[bass.ds(n - 1, 1)].rearrange("q (c t) (b a) -> b (q c) t a", t=TC, a=NA)
                        for b in range(NB):
                            sp.dma_start(dst[b], hst[b * B:(b + 1) * B].rearrange("c j t a -> c (j t) a")).then_inc(c_hst, 16)
                    if has(k - 1):
                        n = k - 1
                        sp.wait_ge(c_dev, (n + 1) * 2)
                        r0 = rows_of(n)
                        dst = rs_d[bass.ds(r0 * P, tiles(n) * P)].rearrange("(i p) d -> p i d", p=P)
                        sp.dma_start(dst, r_o[:, 0:tiles(n), :]).then_inc(c_ro, 16)

                iterate(sp, body)
                sp.wait_ge(c_ro, 16 * (NCH + 1))
                sp.wait_ge(c_wo, 32 * NCH)

            @block.gpsimd
            def _(gp):
                ch = Chain(gp, c_p)
                gp.wait_ge(c_cst, 1)

                def link(ins):
                    ch.link(ins)
                    apart(gp, c_sep)

                TT, TS = nc.gpsimd.tensor_tensor, nc.gpsimd.tensor_scalar
                link(nc.gpsimd.memset(pwc[:, 0, :], -0.5))
                link(nc.gpsimd.memset(pwc[:, 1, :], 0.5))

                def body(k):
                    if has(k + 1):
                        n = k + 1
                        gp.wait_ge(c_st2, n + 1)
                        at_least(gp, c_xf2, n)
                        at_least(gp, c_prom, n)
                        apart(gp, c_sep)
                        link(TS(sc[:, 0, :], mv[:, 0, :, 1], EPS, None, ALU.add))
                        link(TT(sc[:, 1, :], sc[:, 0, :], pwc[:, 0, :], ALU.pow))
                        link(TT(sc[:, 2, :], sc[:, 1, :], sc[:, 1, :], ALU.mult))
                        link(TT(sc[:, 2, :], sc[:, 2, :], mv[:, 0, :, 1], ALU.mult))
                        link(TS(sc[:, 2, :], sc[:, 2, :], EPS, None, ALU.add))
                        link(TT(sc[:, 3, :], sc[:, 2, :], pwc[:, 0, :], ALU.pow))
                        link(TT(sc[:, 4, :], sc[:, 2, :], pwc[:, 1, :], ALU.pow))
                        link(TS(sc[:, 4, :], sc[:, 4, :], SXW, None, ALU.mult))
                        link(TT(sc[:, 3, :], sc[:, 3, :], sc[:, 1, :], ALU.mult))
                        TS(sc[:, 3, :], sc[:, 3, :], SX, None, ALU.mult).then_inc(c_pw2, 1)
                    if has(k - 1):
                        n = k - 1
                        gp.wait_ge(c_sl, n + 1)
                        gp.wait_ge(c_hi3, n + 1)
                        gp.wait_ge(c_lo3, n + 1)
                        apart(gp, c_sep)
                        for i in range(tiles(n)):
                            for c in range(2):
                                nc.gpsimd.indirect_dma_start(
                                    out=xs_d, out_offset=bass.IndirectOffsetOnAxis(ap=sl[:, i, c:c + 1], axis=0),
                                    in_=x3r[:, i].rearrange("p h d -> p (h d)"), in_offset=None,
                                ).then_inc(c_sca, 32 // tiles(n))
                    if has(k):
                        n = k
                        gp.wait_ge(c_st3, n + 1)
                        at_least(gp, c_xf3, n)
                        apart(gp, c_sep)
                        link(TS(sc[:, 5, :], mv[:, 1, :, 1], EPS, None, ALU.add))
                        link(TT(sc[:, 6, :], sc[:, 5, :], pwc[:, 0, :], ALU.pow))
                        TS(sc[:, 6, :], sc[:, 6, :], SX, None, ALU.mult).then_inc(c_pw3, 1)

                iterate(gp, body, ch, PER_POOL)
                gp.wait_ge(c_cst, 3)
                for e in range(E):
                    nc.gpsimd.indirect_dma_start(
                        out=xs_d, out_offset=bass.IndirectOffsetOnAxis(ap=zi[:, e:e + 1], axis=0),
                        in_=zrow[:], in_offset=None).then_inc(c_sca, 16)
                gp.wait_ge(c_sca, 64 * (NCH + 1) + 16 * E)

            @block.tensor
            def _(pe):
                MM = nc.tensor.matmul

                def split3(dst, stat_of, mov_of, steps):
                    last = None
                    parts = [(0, 0), (0, 1), (1, 0)]
                    for s_, step in enumerate(steps):
                        for a, b in parts:
                            last = MM(dst, stat_of(step, a), mov_of(step, b),
                                      start=(s_ == 0 and a + b == 0), stop=(s_ == len(steps) - 1 and a == 1))
                    return last

                def body(k):
                    if has(k - 1):
                        n, w = k - 1, cols(k - 1)
                        pe.wait_ge(c_e3, (n + 1) * 2)
                        at_least(pe, c_toke, clampc(k + 1) * 2)
                        for m in range(SHM + 1):
                            at_least(pe, c_gm, n * 6 + m - 1)
                            bank = BU[m % 2]
                            if m < SHM:
                                for g in range(2):
                                    c0 = g * SHM * P + m * P
                                    last = split3(bank[:, g * TOK:g * TOK + w], lambda s_, a: wsgu[:, s_, a, c0:c0 + P],
                                                  lambda s_, b: x3T[:, b, s_, 0:w], range(KD))
                            else:
                                last = split3(bank[:, 0:w], lambda s_, a: wsgu[:, s_, a, 2 * SHM * P:2 * HS],
                                              lambda s_, b: x3T[:, b, s_, 0:w], range(KD))
                            last.then_inc(c_up, 1)
                            if m == 2:
                                pe.wait_ge(c_m, n + 1)
                                MM(BS[:, 256:256 + 2 * E], tri[:], m16[:].rearrange("p i e -> p (i e)"), start=True, stop=True)
                                MM(BS[:, 288:288 + 2 * E], ones16[:], m16[:].rearrange("p i e -> p (i e)"),
                                   start=True, stop=True).then_inc(c_rk, 1)
                    if has(k - 1):
                        pe.wait_ge(c_gl, k * 6)
                    for i in range(2):
                        if has(k - 1) and i < tiles(k - 1):
                            n = k - 1
                            at_least(pe, c_dev, n * 2 + i)
                            t = slice(i * P, (i + 1) * P)
                            for m in range(SHM + 1):
                                p0 = 0 if m < SHM else SHT
                                for a, b in ((0, 0), (0, 1), (1, 0)):
                                    last = MM(BD[:], gT[p0:P, m, a, t], wsd[p0:P, m, b, :], start=(m == 0 and a + b == 0),
                                              stop=(m == SHM and a == 1))
                            last.then_inc(c_dn, 2 // tiles(n))
                        if has(k) and i < tiles(k):
                            n = k
                            if i == 0:
                                pe.wait_ge(c_yh, n + 1)
                                pe.wait_ge(c_yl, n + 1)
                                at_least(pe, c_sl, n)
                            at_least(pe, c_oev, n * 2 + i)
                            t = slice(i * P, (i + 1) * P)
                            split3(BS[:], lambda s_, a: x2T[:, a, s_, t], lambda s_, b: wskip[:, s_, b, :], range(KD))
                            MM(BY[:], yT[:, 0, t], wout[:, 0, :], start=True, stop=False)
                            MM(BY[:], yT[:, 0, t], wout[:, 1, :], start=False, stop=False)
                            MM(BY[:], yT[:, 1, t], wout[:, 0, :], start=False, stop=False)
                            MM(BY[:], ones_row[:], brow[:, 0, :], start=False, stop=False)
                            MM(BY[:], ones_row[:], brow[:, 1, :], start=False, stop=True).then_inc(c_out, 2 // tiles(n))
                    if htok(k + 2):
                        n = k + 2
                        pe.wait_ge(c_tokp, n)
                        if k >= 1 or not isinstance(k, int):
                            pe.wait_ge(c_gm, k * 6)
                        for j in range(JC):
                            o = j % 4 * 2 * NA
                            for f in range(2):
                                last = MM(BU[j // 4][:, o:o + 2 * NA], pp[:, f, j].rearrange("p b c -> p (b c)"),
                                          ea[:, f, j].rearrange("p t a -> p (t a)"), start=(f == 0), stop=(f == 1))
                        last.then_inc(c_tokm, 1)
                    if has(k + 1):
                        n = k + 1
                        pe.wait_ge(c_hi2, n + 1)
                        pe.wait_ge(c_lo2, n + 1)
                        if has(k - 1):
                            pe.wait_ge(c_dev, k * 2)
                        at_least(pe, c_e3, n * 2 - 2)
                        for i in range(tiles(n)):
                            bank = BX[i][:].bitcast(F16)
                            for h in range(2):
                                for c in range(KD):
                                    last = nc.tensor.transpose(bank[:, (h * KD + c) * P:(h * KD + c + 1) * P],
                                                               x2r[:, i, h, c * P:(c + 1) * P], ident16[:])
                            last.then_inc(c_t2, 2 // tiles(n))
                        w = cols(n)
                        pe.wait_ge(c_e2, (n + 1) * 2)
                        at_least(pe, c_yf, n)
                        for m in range(3):
                            dst = (BG[:, 0:w], BB[:, 0:w], BG[:, TOK:TOK + w])[m]
                            last = split3(dst, lambda s_, a: win[:, s_, a, m * S:(m + 1) * S],
                                          lambda s_, b: x2T[:, b, s_, 0:w], range(KD))
                        last.then_inc(c_gt, 1)
                    if has(k):
                        n = k
                        pe.wait_ge(c_hi3, n + 1)
                        pe.wait_ge(c_lo3, n + 1)
                        for i in range(tiles(n)):
                            bank = BX[i][:].bitcast(F16)
                            if has(k + 1):
                                pe.wait_ge(c_e2, (k + 2) * 2)
                            for h in range(2):
                                for c in range(KD):
                                    last = nc.tensor.transpose(bank[:, (h * KD + c) * P:(h * KD + c + 1) * P],
                                                               x3r[:, i, h, c * P:(c + 1) * P], ident16[:])
                            last.then_inc(c_t3, 2 // tiles(n))
                        pe.wait_ge(c_e3, (n + 1) * 2)
                        pe.wait_ge(c_oev, (n + 1) * 2)
                        for i in range(tiles(n)):
                            t = slice(i * P, (i + 1) * P)
                            last = split3(BS[:, i * E:(i + 1) * E], lambda s_, a: x3T[:, a, s_, t],
                                          lambda s_, b: gw[:, s_, b, :], range(KD))
                        last.then_inc(c_rt, 1)

                pe.wait_ge(c_cst, 2)
                iterate(pe, body)

            @block.scalar
            def _(act):
                A = nc.scalar.activation

                def silu(n, m):
                    w = cols(n)
                    act.wait_ge(c_up, n * 6 + m + 1)
                    at_least(act, c_gm, n * 6 + m - 1)
                    p1 = P if m < SHM else SHT
                    A(sgs[P - p1:P, m % 2, 0:w], BU[m % 2][0:p1, 0:w], ACT.Silu, scale=SXW).then_inc(c_sg, 1)

                def ghigh(n, m):
                    w, p0 = cols(n), (0 if m < SHM else SHT)
                    act.wait_ge(c_gm, n * 6 + m + 1)
                    at_least(act, c_dn, n * 2)
                    A(gT[p0:P, m, 0, 0:w], gf[p0:P, m % 2, 0:w], ACT.Copy).then_inc(c_gh, 1)

                def body(k):
                    if has(k):
                        n, w, nt = k, cols(k), tiles(k)
                        act.wait_ge(c_hx, (n + 1) * 16)
                        act.wait_ge(c_pw2, n + 1)
                        at_least(act, c_oev, n * 2)
                        A(ir[:], sc[:, 4, :], ACT.Copy).then_inc(c_irc, 1)
                        A(hc[:, 0:nt, :], hx[:, 0:nt, :], ACT.Copy).then_inc(c_prom, 1)
                        act.wait_ge(c_gt, n + 1)
                        A(th[:, 0:w], BG[:, 0:w], ACT.Tanh, bias=cbh[:, 0:1], scale=0.5 * SXW)
                        A(tc[:, 0:w], BG[:, TOK:TOK + w], ACT.Tanh, bias=cb[:, 2:3], scale=SXW).then_inc(c_th, 1)
                    if has(k - 1):
                        silu(k - 1, 0)
                    if has(k):
                        act.wait_ge(c_yf, k + 1)
                        at_least(act, c_out, k * 2)
                        A(yT[:, 0, 0:cols(k)], hsc[:, 0:cols(k)], ACT.Copy).then_inc(c_yh, 1)
                    if has(k - 1):
                        n = k - 1
                        silu(n, 1)
                        ghigh(n, 0)
                        for m in range(2, SHM + 1):
                            silu(n, m)
                            ghigh(n, m - 1)
                        ghigh(n, SHM)
                    if has(k + 1):
                        n, nt = k + 1, tiles(k + 1)
                        act.wait_ge(c_xf2, n + 1)
                        at_least(act, c_t2, n * 2)
                        A(x2r[:, 0:nt, 0, :], xf[:, 0:nt, :], ACT.Copy).then_inc(c_hi2, 1)
                    if htok(k + 2):
                        n = k + 2
                        act.wait_ge(c_tokm, n)
                        at_least(act, c_hst, (n - 1) * NB * 16)
                        for t in range(2):
                            A(hst[:, t * 4:t * 4 + 4].rearrange("p j t a -> p (j t a)"), BU[t][:], ACT.Copy).then_inc(c_toke, 1)
                    if has(k + 1):
                        n, nt = k + 1, tiles(k + 1)
                        at_least(act, c_out, (k + 1) * 2)
                        for i in range(nt):
                            act.wait_ge(c_t2, n * 2 + (i + 1) * 2 // nt)
                            A(x2T[:, :, :, i * P:(i + 1) * P].rearrange("p h k t -> p (h k) t"),
                              BX[i][:].bitcast(F16).rearrange("p (c t) -> p c t", t=P), ACT.Copy).then_inc(c_e2, 2 // nt)
                    if has(k):
                        n, nt = k, tiles(k)
                        act.wait_ge(c_xf3, n + 1)
                        at_least(act, c_sca, n * 64)
                        A(x3r[:, 0:nt, 0, :], xf[:, 0:nt, :], ACT.Copy).then_inc(c_hi3, 1)
                        if htok(k):
                            act.wait_ge(c_wi, k * 64)
                            at_least(act, c_wo, k * 32 - 32)
                            for g in range(2):
                                A(hgu[:, :, 0, g * H:(g + 1) * H], rgu[:, g], ACT.Copy, scale=SW)
                            A(hdn[:, 0:2, 0, :], rdn[:, 0:2, :], ACT.Copy, scale=SW)
                            A(hdn[0:HK[2], 2, 0, :], rdn[0:HK[2], 2, :], ACT.Copy, scale=SW).then_inc(c_wh, 1)
                        for i in range(nt):
                            act.wait_ge(c_t3, n * 2 + (i + 1) * 2 // nt)
                            A(x3T[:, :, :, i * P:(i + 1) * P].rearrange("p h k t -> p (h k) t"),
                              BX[i][:].bitcast(F16).rearrange("p (c t) -> p c t", t=P), ACT.Copy).then_inc(c_e3, 2 // nt)

                act.wait_ge(c_cst, 2)
                iterate(act, body)

            @block.vector
            def _(v):
                ch = Chain(v, c_v)
                link = ch.link
                TT, TS, STT = nc.vector.tensor_tensor, nc.vector.tensor_scalar, nc.vector.scalar_tensor_tensor
                RED = nc.vector.tensor_reduce

                def tok_e(n, part):
                    j = bass.ds((n - 1) * JC, JC)
                    shape = [P, JC, NB, NB]
                    gq = lambda r: pg[:, r, :, j].rearrange("p q (j o) -> p j q o", o=1).broadcast_to(shape)
                    er = lambda r: pe_[:, r, :, j].rearrange("p (o r) j -> p j o r", o=1).broadcast_to(shape)
                    o = lambda t: t.rearrange("p j (q r) -> p j q r", r=NB)
                    if part < 4:
                        ins = TT(o(et[:, part]), gq((0, 1, 0, 1)[part]), er((0, 1, 1, 0)[part]), ALU.mult)
                        if part < 3:
                            ch.do(ins)
                        else:
                            link(ins)
                    else:
                        at_least(v, c_tokm, n - 1)
                        for t in range(2):
                            q = slice(t * N, (t + 1) * N)
                            ch.do(TT(ea[q, 0, :, t, :], et[q, 0], et[q, 1], ALU.subtract))
                            ch.do(STT(ea[q, 1, :, t, :], et[q, 2], -1.0, et[q, 3], ALU.mult, ALU.subtract))

                def tok_p(n, f):
                    if f < 4:
                        j = bass.ds((n - 1) * JC, JC)
                        shape = [P, JC, NB, B]
                        c_, h_ = ((0, 0), (1, 1), (0, 1), (1, 0))[f]
                        cc = cT[:, c_, :, j].rearrange("p (o c) j -> p j o c", o=1).broadcast_to(shape)
                        hh = ph[:, h_, :, j].rearrange("p b (j o) -> p j b o", o=1).broadcast_to(shape)
                        if f == 0:
                            at_least(v, c_tokm, n - 1)
                        ch.do(TT((pp, pt)[f % 2][:, f // 2], cc, hh, ALU.mult))
                        if f == 3:
                            ch.sync()
                    else:
                        fl = lambda t: t[:, f - 4].rearrange("p j b c -> p (j b c)")
                        ins = TT(fl(pp), fl(pp), fl(pt), ALU.subtract if f == 4 else ALU.add)
                        if f == 5:
                            ch.sync()
                            ins.then_inc(c_tokp, 1)
                        else:
                            ch.do(ins)

                def glow(n, m):
                    w, p0 = cols(n), (0 if m < SHM else SHT)
                    v.wait_ge(c_gh, n * 6 + m + 1)
                    TT(gT[p0:P, m, 1, 0:w], gf[p0:P, m % 2, 0:w], gT[p0:P, m, 0, 0:w], ALU.subtract).then_inc(c_gl, 1)

                def gprod(n, m):
                    w, p0 = cols(n), (0 if m < SHM else SHT)
                    v.wait_ge(c_sg, n * 6 + m + 1)
                    at_least(v, c_gl, n * 6 + m - 1)
                    u = BU[m % 2][:, TOK:TOK + w] if m < SHM else BU[m % 2][SHT:P, 0:w]
                    STT(gf[p0:P, m % 2, 0:w], u, SXW, sgs[p0:P, m % 2, 0:w], ALU.mult, ALU.mult).then_inc(c_gm, 1)

                def choose(n):
                    nt = tiles(n)
                    r = lambda i: rt[:, i, 0:nt, :]
                    q = lambda i: rm[:, i, 0:nt]
                    wide = lambda i: rm[:, i, 0:nt].rearrange("p (i o) -> p i o", o=1).broadcast_to([P, nt, E])
                    f = lambda ap: ap.rearrange("p i e -> p (i e)")
                    v.wait_ge(c_rt, n + 1)
                    link(TS(f(r(0)), BS[:, 0:nt * E], SXW, None, ALU.mult))
                    ch.do(nc.vector.tensor_copy(logits[:, bass.ds(rows_of(n), nt), :], r(0)))
                    for c in range(2):
                        link(RED(q(c), r(0), AX.X, ALU.max))
                        link(TT(r(1), r(0), wide(c), ALU.is_equal))
                        link(TT(r(1), r(1), rev[:, 0:nt, :], ALU.mult))
                        link(RED(q(2 + c), r(1), AX.X, ALU.max))
                        link(TT(oh[:, c, 0:nt, :], r(1), wide(2 + c), ALU.is_equal))
                        if c == 0:
                            link(STT(f(r(0)), f(oh[:, 0, 0:nt, :]), -3e38, f(r(0)), ALU.mult, ALU.add))
                    ch.do(nc.vector.tensor_copy(top_l[:, bass.ds(rows_of(n), nt), :],
                                                rm[:, 0:2, 0:nt].rearrange("p c i -> p i c")))
                    if nt == 1:
                        link(TS(oh[:, :, 0, :], oh[:, :, 0, :], mask0[:, 0:1], None, ALU.mult))
                    TT(m16[:, 0:nt, :], oh[:, 0, 0:nt, :], oh[:, 1, 0:nt, :], ALU.add).then_inc(c_m, 1)

                def place(n):
                    nt = tiles(n)
                    v.wait_ge(c_rk, n + 1)
                    at_least(v, c_sca, n * 64)
                    for i in range(nt):
                        link(TT(rt[:, 2, i, :], BS[:, 256 + i * E:256 + (i + 1) * E], run[:], ALU.add))
                        link(TT(run[:], BS[:, 288 + i * E:288 + (i + 1) * E], run[:], ALU.add))
                    for c in range(2):
                        link(TT(rt[:, 3, 0:nt, :], oh[:, c, 0:nt, :], rt[:, 2, 0:nt, :], ALU.mult))
                        link(RED(rm[:, 4 + c, 0:nt], rt[:, 3, 0:nt, :], AX.X, ALU.add))
                    both = rm[:, 4:6, 0:nt].rearrange("p c i -> p i c")
                    dst = slots[:, bass.ds(rows_of(n), nt), :]
                    if nt == 1:
                        link(TT(rm[:, 7, :], rm[:, 4:6, 0], dump_s[:], ALU.add))
                        ch.do(nc.vector.tensor_copy(slots[:, 0, :], rm[:, 4:6, 0]))
                        nc.vector.tensor_copy(sl[:, 0, :], rm[:, 7, :]).then_inc(c_sl, 1)
                    else:
                        ch.do(nc.vector.tensor_copy(dst, both))
                        nc.vector.tensor_copy(sl[:], both).then_inc(c_sl, 1)

                def body(k):
                    if has(k):
                        n, w = k, cols(k)
                        nb = w // TC
                        v.wait_ge(c_th, n + 1)
                        ch.do(TS(om[:, 0:w], th[:, 0:w], -0.5, 0.5, ALU.mult, ALU.add))
                        ch.do(TS(al[:, 0:w], th[:, 0:w], 0.5, 0.5, ALU.mult, ALU.add))
                        link(TS(bb[:, 0:w], BB[:, 0:w], SXW, cb[:, 1:2], ALU.mult, ALU.add))
                        link(TT(bb[:, 0:w], bb[:, 0:w], al[:, 0:w], ALU.mult))
                        first = lambda t: t[:, 0:w].rearrange("p (c t) -> p c t", t=TC)[:, :, 0]
                        link(TT(fix[:, 0:nb], first(om), carry[:, 0:nb], ALU.mult))
                        link(TT(first(bb), first(bb), fix[:, 0:nb], ALU.add))
                        link(nc.vector.memset(first(om), 0.0))
                        link(nc.vector.tensor_tensor_scan(al[:, 0:w], om[:, 0:w], bb[:, 0:w], 0.0, ALU.mult, ALU.add))
                        if nb < B:
                            link(nc.vector.tensor_copy(carry[:], al[:, 0:1].broadcast_to([P, B])))
                        else:
                            link(nc.vector.tensor_copy(carry[:], al[:, 0:w].rearrange("p (c t) -> p c t", t=TC)[:, :, TC - 1]))
                        at_least(v, c_yl, n)
                        STT(hsc[:, 0:w], al[:, 0:w], SY, tc[:, 0:w], ALU.mult, ALU.mult).then_inc(c_yf, 1)
                    if has(k - 1):
                        gprod(k - 1, 0)
                    if has(k):
                        v.wait_ge(c_yh, k + 1)
                        TT(yT[:, 1, 0:cols(k)], hsc[:, 0:cols(k)], yT[:, 0, 0:cols(k)], ALU.subtract).then_inc(c_yl, 1)
                    if has(k - 1):
                        choose(k - 1)
                        gprod(k - 1, 1)
                    if has(k + 1):
                        n, nt = k + 1, tiles(k + 1)
                        v.wait_ge(c_hx, (n + 1) * 16)
                        for i in range(nt):
                            ch.do(nc.vector.bn_stats(stat[:, 0, i, :], hx[:, i, :]))
                        ch.sync()
                        apart(v, c_sep)
                        if nt == 1:
                            ch.do(nc.vector.memset(mv[:], 1.0))
                            ch.sync()
                        for i in range(nt):
                            last = nc.vector.bn_aggr(mv[:, 0, i, :], stat[:, 0, i, :])
                        last.then_inc(c_st2, 1)
                    for m in range(5):
                        if htok(k + 2):
                            tok_e(k + 2, m)
                        if has(k - 1):
                            glow(k - 1, m)
                            if m < 4:
                                gprod(k - 1, m + 2)
                    if has(k - 1):
                        place(k - 1)
                        glow(k - 1, 5)
                    if has(k + 1):
                        n, nt = k + 1, tiles(k + 1)
                        v.wait_ge(c_pw2, n + 1)
                        at_least(v, c_hi3, n - 1)
                        for i in range(nt):
                            last = TS(xf[:, i, :], hx[:, i, :], mv[:, 0, i, 0:1], sc[:, 3, i:i + 1], ALU.subtract, ALU.mult)
                        last.then_inc(c_xf2, 1)
                        v.wait_ge(c_hi2, n + 1)
                        TT(x2r[:, 0:nt, 1, :], xf[:, 0:nt, :], x2r[:, 0:nt, 0, :], ALU.subtract).then_inc(c_lo2, 1)
                    if htok(k + 2):
                        tok_p(k + 2, 0)
                    for i in range(2):
                        if has(k - 1) and i < tiles(k - 1):
                            n, nt = k - 1, tiles(k - 1)
                            v.wait_ge(c_dn, n * 2 + (i + 1) * 2 // nt)
                            at_least(v, c_ro, n * 16)
                            STT(r_o[:, i, :], BD[:], 1.0 / SW, h2[:, i, :], ALU.mult, ALU.add).then_inc(c_dev, 2 // nt)
                        if htok(k + 2):
                            for f in ((1, 2), (4, 5))[i]:
                                tok_p(k + 2, f)
                        if has(k) and i < tiles(k):
                            n, nt = k, tiles(k)
                            v.wait_ge(c_out, n * 2 + (i + 1) * 2 // nt)
                            v.wait_ge(c_prom, n + 1)
                            if has(k - 1):
                                v.wait_ge(c_dev, (k - 1) * 2 + (2 if tiles(k - 1) == 1 else i + 1))
                            link(STT(h2[:, i, :], BS[:], ir[:, i:i + 1], hc[:, i, :], ALU.mult, ALU.add))
                            STT(h2[:, i, :], BY[:], 1.0 / (SW * SY), h2[:, i, :], ALU.mult, ALU.add).then_inc(c_oev, 2 // nt)
                            v.wait_ge(c_oev, n * 2 + (i + 1) * 2 // nt)
                            link(nc.vector.bn_stats(stat[:, 1, i, :], h2[:, i, :]))
                            apart(v, c_sep)
                            last = nc.vector.bn_aggr(mv[:, 1, i, :], stat[:, 1, i, :])
                            if i == nt - 1:
                                last.then_inc(c_st3, 1)
                            else:
                                ch.do(last)
                        if htok(k + 2) and i == 0:
                            tok_p(k + 2, 3)
                    if has(k):
                        n, nt = k, tiles(k)
                        v.wait_ge(c_pw3, n + 1)
                        if has(k + 1):
                            v.wait_ge(c_lo2, k + 2)
                        for i in range(nt):
                            last = TS(xf[:, i, :], h2[:, i, :], mv[:, 1, i, 0:1], sc[:, 6, i:i + 1], ALU.subtract, ALU.mult)
                        last.then_inc(c_xf3, 1)
                        v.wait_ge(c_hi3, n + 1)
                        TT(x3r[:, 0:nt, 1, :], xf[:, 0:nt, :], x3r[:, 0:nt, 0, :], ALU.subtract).then_inc(c_lo3, 1)
                    if htok(k):
                        v.wait_ge(c_wh, k)
                        for g in range(2):
                            STT(hgu[:, :, 1, g * H:(g + 1) * H], rgu[:, g], SW, hgu[:, :, 0, g * H:(g + 1) * H], ALU.mult, ALU.subtract)
                        STT(hdn[:, 0:2, 1, :], rdn[:, 0:2, :], SW, hdn[:, 0:2, 0, :], ALU.mult, ALU.subtract)
                        STT(hdn[0:HK[2], 2, 1, :], rdn[0:HK[2], 2, :], SW, hdn[0:HK[2], 2, 0, :], ALU.mult,
                            ALU.subtract).then_inc(c_wl, 1)

                ch.do(nc.vector.memset(carry[:], 0.0))
                link(nc.vector.memset(ea[:].rearrange("p f j t a -> p (f j t a)"), 0.0))
                nc.vector.memset(hdn[HK[2]:P, 2, :, :], 0.0).then_inc(c_cst, 1)
                nc.vector.memset(m16[:], 0.0).then_inc(c_cst, 1)
                v.wait_ge(c_cst, 2)
                iterate(v, body, ch, PER_DVE)
                v.wait_ge(c_sl, NCH + 1)
                TS(zi[:], run[:], pcol[:, 0:1], None, ALU.add).then_inc(c_cst, 1)

        phase1.close()

        wts = keep("wts", [P, TILES, 2], F32)
        tbl = keep("tbl", [P, 3, NSLOT], I32)
        with ExitStack() as ph2:
            t2 = sb_in(ph2)
            wexp = t2("wexp", [P, 2 * E, UW], F16)
            xr = [t2(f"xr{b}", [P, 2, D], F16) for b in range(2)]
            yo = [t2(f"yo{b}", [P, D], F32) for b in range(2)]
            xT = t2("xT", [P, 2, KD, P], F16)
            sg = t2("sg", [P, H], F32)
            gx = t2("gx", [P, H], F32)
            gh = t2("gh", [P, 2, H], F16)
            gT2 = t2("gT2", [P, 2, KH, P], F16)
            io1 = t2("io1", [P, TILES], I32)
            io2 = t2("io2", [P, NSLOT], I32)
            jf = t2("jf", [P, TILES], F32)
            jn = t2("jn", [P, NSLOT], F32)
            cmp1 = t2("cmp1", [P, E, TILES], F32)
            cmp2 = t2("cmp2", [P, NSLOT, E], F32)
            cmp3 = t2("cmp3", [P, NSLOT, E], F32)
            used = t2("used", [P, 3, E], F32)
            jt = t2("jt", [P, 6, NSLOT], F32)
            lx = t2("lx", [P, TILES, E + 1], F32)
            lt = t2("lt", [P, TILES], F32)
            rg = t2("rg", [P, TILES, 2], F32)
            rh = t2("rh", [P, TILES, 2], F32)

            XB, GB, UB, TB, DB = psum[0], psum[1], psum[2], psum[3], psum[4]

            d_w = sem("d_w")
            d_tb = sem("d_tb")
            d_io = sem("d_io")
            d_lx = sem("d_lx")
            d_xl = [sem("d_xl0"), sem("d_xl1")]
            d_ys = [sem("d_ys0"), sem("d_ys1")]
            d_xt = sem("d_xt")
            d_xe = sem("d_xe")
            d_gu = sem("d_gu")
            d_sg = sem("d_sg")
            d_gf = sem("d_gf")
            d_gh = sem("d_gh")
            d_gl = sem("d_gl")
            d_gt = sem("d_gt")
            d_ge = sem("d_ge")
            d_dn = sem("d_dn")
            d_ye = sem("d_ye")
            d_sep = sem("d_sep")
            d_v = sem("d_v")

            def over_tiles(eng, body):
                for b in range(2):
                    body(b, b)
                with eng.Fori(1, NSLOT // 2 - 1) as ii:
                    for b in range(2):
                        body(ii * 2 + b, b)
                for b in range(2):
                    body(NSLOT - 2 + b, b)

            at_end = lambda i: isinstance(i, int) and i >= NSLOT
            halfcount = lambda i, b: (i - b) * 8 + 16

            block = ph2.enter_context(nc.Block())

            @block.gpsimd
            def _(gp):
                nc.gpsimd.iota(io1[:], pattern=[[P, TILES]], base=0, channel_multiplier=0).then_inc(d_io, 1)
                nc.gpsimd.iota(io2[:], pattern=[[1, NSLOT]], base=0, channel_multiplier=0).then_inc(d_io, 1)
                for e in range(E):
                    at_least(gp, d_w, 16 * e)
                    gp.dma_start(wexp[:, 2 * e:2 * e + 2, :], w16_d[2 * e:2 * e + 2].rearrange("u p n -> p u n")).then_inc(d_w, 16)
                gp.wait_ge(d_w, 16 * E)

            @block.sync
            def _(sp):
                def load(i, b):
                    row = sp.value_load(tbl[0:1, 1, bass.ds(i, 1)], min_val=0, max_val=NR - P)
                    sp.dma_start(xr[b][:].rearrange("p h d -> p (h d)"), xs_d[bass.ds(row, P), :]).then_inc(d_xl[b], 16)

                def body(i, b):
                    if not at_end(i + 2):
                        sp.wait_ge(d_xt, i + 1)
                        load(i + 2, b)
                    sp.wait_ge(d_ye, i + 1)
                    sp.dma_start(ys_d[bass.ds(i * P, P), :], yo[b][:]).then_inc(d_ys[b], 16)

                sp.wait_ge(d_tb, 1)
                for b in range(2):
                    load(b, b)
                over_tiles(sp, body)
                for b in range(2):
                    sp.wait_ge(d_ys[b], 16 * (NSLOT // 2))

            @block.tensor
            def _(pe):
                MM = nc.tensor.matmul
                X16, T16 = XB[:].bitcast(F16), TB[:].bitcast(F16)

                def rows_T(i, b):
                    pe.wait_ge(d_xl[b], halfcount(i, b))
                    at_least(pe, d_xe, i)
                    for h in range(2):
                        for c in range(KD):
                            last = nc.tensor.transpose(X16[:, (h * KD + c) * P:(h * KD + c + 1) * P],
                                                       xr[b][:, h, c * P:(c + 1) * P], ident16[:])
                    last.then_inc(d_xt, 1)

                def gate_up(i, unit):
                    pe.wait_ge(d_xe, i + 1)
                    at_least(pe, d_gf, i)
                    for c in range(KD):
                        for a, w in ((0, 0), (0, 1), (1, 0)):
                            u, o = bass.ds(unit + c // 2, 1), (c % 2 * 2 + w) * 2 * H
                            s_, e_ = (c == 0 and a + w == 0), (c == KD - 1 and a == 1)
                            MM(GB[:, 0:H], xT[:, a, c, :], wexp[:, u, o:o + H], start=s_, stop=e_)
                            last = MM(UB[:, 0:H], xT[:, a, c, :], wexp[:, u, o + H:o + 2 * H], start=s_, stop=e_)
                    last.then_inc(d_gu, 1)

                def down(i, unit):
                    pe.wait_ge(d_ge, i + 1)
                    at_least(pe, d_ye, i)
                    for c in range(KH):
                        for a, w in ((0, 0), (0, 1), (1, 0)):
                            o = UG + (c * 2 + w) * (D // 2)
                            last = MM(DB[:], gT2[0:HK[c], a, c, :], wexp[0:HK[c], bass.ds(unit, 2), o:o + D // 2],
                                      start=(c == 0 and a + w == 0), stop=(c == KH - 1 and a == 1))
                    last.then_inc(d_dn, 1)

                def prod_T(i):
                    pe.wait_ge(d_gh, i + 1)
                    pe.wait_ge(d_gl, i + 1)
                    at_least(pe, d_ge, i)
                    for h in range(2):
                        for c in range(KH):
                            last = nc.tensor.transpose(T16[0:HK[c], (h * KH + c) * P:(h * KH + c + 1) * P],
                                                       gh[:, h, c * P:c * P + HK[c]], ident16[:])
                    last.then_inc(d_gt, 1)

                def unit_of(i):
                    apart(pe, d_sep)
                    return pe.value_load(tbl[0:1, 0, bass.ds(i, 1)], min_val=0, max_val=2 * (E - 1))

                def body(i, b):
                    apart(pe, d_sep)
                    count = pe.value_load(tbl[0:1, 2, bass.ds(i, 1)], min_val=16, max_val=16 * E)
                    pe.wait_ge(d_w, count)
                    gate_up(i, unit_of(i))
                    if not at_end(i + 1):
                        rows_T(i + 1, 1 - b)
                    if not isinstance(i, int) or i > 0:
                        down(i - 1, unit_of(i - 1))
                    prod_T(i)

                pe.wait_ge(d_tb, 1)
                rows_T(0, 0)
                over_tiles(pe, body)
                down(NSLOT - 1, unit_of(NSLOT - 1))

            @block.scalar
            def _(act):
                A = nc.scalar.activation

                def rows_out(i):
                    act.wait_ge(d_xt, i + 1)
                    at_least(act, d_gu, i)
                    A(xT[:].rearrange("p h k t -> p (h k t)"), XB[:].bitcast(F16), ACT.Copy).then_inc(d_xe, 1)

                def body(i, b):
                    act.wait_ge(d_gu, i + 1)
                    A(sg[:], GB[:, 0:H], ACT.Silu, scale=SXW).then_inc(d_sg, 1)
                    act.wait_ge(d_gf, i + 1)
                    at_least(act, d_gt, i)
                    A(gh[:, 0, :], gx[:], ACT.Copy).then_inc(d_gh, 1)
                    if not at_end(i + 1):
                        rows_out(i + 1)

                act.wait_ge(d_lx, 1)
                A(lx[:], lx[:], ACT.Exp).then_inc(d_lx, 1)
                rows_out(0)
                over_tiles(act, body)

            @block.vector
            def _(v):
                ch = Chain(v, d_v)
                link = ch.link
                TT, TS, STT = nc.vector.tensor_tensor, nc.vector.tensor_scalar, nc.vector.scalar_tensor_tensor
                RED = nc.vector.tensor_reduce
                v.wait_ge(d_io, 2)
                ch.do(nc.vector.tensor_copy(jf[:], io1[:]))
                link(nc.vector.tensor_copy(jn[:], io2[:]))
                link(TS(used[:, 0, :], rev[:, 0, :], float(CAP), -float(CAP * E), ALU.mult, ALU.add))
                link(TT(used[:, 0, :], run[:], used[:, 0, :], ALU.add))
                e_by = lambda ap, n: ap.rearrange("p (e o) -> p e o", o=1).broadcast_to([P, E, n])
                link(TT(cmp1[:], e_by(used[:, 0, :], TILES), jf[:].rearrange("p (o j) -> p o j", o=1).broadcast_to([P, E, TILES]),
                        ALU.is_gt))
                link(RED(used[:, 1, :], cmp1[:], AX.X, ALU.add))
                link(nc.vector.memset(used[:, 0, :], 1.0))
                link(nc.vector.tensor_tensor_scan(used[:, 2, :], used[:, 0, :], used[:, 1, :], 0.0, ALU.mult, ALU.add))
                by_j = lambda ap: ap.rearrange("p (o e) -> p o e", o=1).broadcast_to([P, NSLOT, E])
                link(TT(cmp2[:], jn[:].rearrange("p (j o) -> p j o", o=1).broadcast_to([P, NSLOT, E]), by_j(used[:, 2, :]), ALU.is_ge))
                link(RED(jt[:, 0, :], cmp2[:], AX.X, ALU.add))
                link(TT(cmp3[:], cmp2[:], by_j(used[:, 1, :]), ALU.mult))
                link(RED(jt[:, 1, :], cmp3[:], AX.X, ALU.add))
                link(TS(jt[:, 2, :], jt[:, 0, :], float(E), None, ALU.is_lt))
                link(TT(jt[:, 3, :], jn[:], jt[:, 1, :], ALU.subtract))
                link(TS(jt[:, 3, :], jt[:, 3, :], float(P), None, ALU.mult))
                link(STT(jt[:, 3, :], jt[:, 0, :], float(CAP), jt[:, 3, :], ALU.mult, ALU.add))
                link(TT(jt[:, 0, :], jt[:, 0, :], jt[:, 2, :], ALU.mult))
                link(TS(tbl[:, 0, :], jt[:, 0, :], 2.0, None, ALU.mult))
                link(TS(tbl[:, 2, :], jt[:, 0, :], 16.0, 16.0, ALU.mult, ALU.add))
                link(TS(jt[:, 4, :], jt[:, 3, :], -float(ZERO), None, ALU.add))
                link(TT(jt[:, 4, :], jt[:, 4, :], jt[:, 2, :], ALU.mult))
                TS(tbl[:, 1, :], jt[:, 4, :], float(ZERO), None, ALU.add).then_inc(d_tb, 1)
                link(TS(used[:, 0, :], used[:, 1, :], float(P), -float(CAP), ALU.mult, ALU.add))
                link(nc.vector.tensor_copy(rg[:], slots[:]))
                for e in range(E - 1):
                    link(TS(rh[:], slots[:], float((e + 1) * CAP), used[:, 0, e:e + 1], ALU.is_ge, ALU.mult))
                    link(TT(rg[:], rg[:], rh[:], ALU.add))
                link(nc.vector.tensor_copy(rows_y[:, 0:TILES, :], rg[:]))
                wide = lambda ap: ap.broadcast_to([P, TILES, E])
                link(TT(lx[:, :, 0:E], logits[:], wide(top_l[:, :, 0:1]), ALU.subtract))
                TT(lx[:, :, E], top_l[:, :, 1], top_l[:, :, 0], ALU.subtract).then_inc(d_lx, 1)
                v.wait_ge(d_lx, 2)
                link(RED(lt[:], lx[:, :, 0:E], AX.X, ALU.add))
                link(nc.vector.reciprocal(wts[:, :, 0], lt[:]))
                link(TT(wts[:, :, 1], wts[:, :, 0], lx[:, :, E], ALU.mult))

                def out_of(i, b):
                    v.wait_ge(d_dn, i + 1)
                    at_least(v, d_ys[b], halfcount(i, b) - 16)
                    TS(yo[b][:], DB[:], 1.0 / SW, None, ALU.mult).then_inc(d_ye, 1)

                def body(i, b):
                    v.wait_ge(d_sg, i + 1)
                    at_least(v, d_gl, i)
                    STT(gx[:], UB[:, 0:H], SXW, sg[:], ALU.mult, ALU.mult).then_inc(d_gf, 1)
                    v.wait_ge(d_gh, i + 1)
                    TT(gh[:, 1, :], gx[:], gh[:, 0, :], ALU.subtract).then_inc(d_gl, 1)
                    if not isinstance(i, int) or i > 0:
                        out_of(i - 1, 1 - b)
                    v.wait_ge(d_gt, i + 1)
                    T16 = TB[:].bitcast(F16)
                    tt = lambda c0, c1: T16[:, 0:2 * KH * P].rearrange("p (h c t) -> p h c t", h=2, c=KH)[:, :, c0:c1, :]
                    nc.vector.tensor_copy(gT2[:, :, 0:KH - 1, :], tt(0, KH - 1))
                    nc.vector.tensor_copy(gT2[0:HK[-1], :, KH - 1:KH, :], tt(KH - 1, KH)[0:HK[-1]]).then_inc(d_ge, 1)

                over_tiles(v, body)
                out_of(NSLOT - 1, 1)

        with ExitStack() as ph3:
            t3 = sb_in(ph3)
            idx = t3("idx", [P, NBUF, 2], I32)
            rr = t3("rr", [P, NBUF, D], F32)
            y1 = t3("y1", [P, NBUF, 2, D], F32)
            e_r = [sem(f"e_r{b}") for b in range(NBUF)]
            e_y = [sem(f"e_y{b}") for b in range(NBUF)]
            e_o = [sem(f"e_o{b}") for b in range(NBUF)]
            e_f = sem("e_f")
            e_i = [sem(f"e_i{b}") for b in range(NBUF)]
            e_sep = sem("e_sep")
            e_m = sem("e_m")
            block = ph3.enter_context(nc.Block())
            assert (TILES - 1) % NBUF == 0
            GR = (TILES - 1) // NBUF

            def before(g, b):
                return g + (1 if b == 0 else 0)

            def run_groups(eng, body):
                body(0, 0, 0, 0)
                for b in range(NBUF):
                    body(b + 1, before(0, b), b, 0)
                with eng.Fori(1, GR) as g:
                    for b in range(NBUF):
                        body(g * NBUF + (b + 1), before(g, b), b, g)

            @block.sync
            def _(sp):
                def body(tile, n, b, g):
                    at_least(sp, e_o[b], n * 16)
                    sp.dma_start(rr[:, b, :], rs_d[bass.ds(tile * P, P), :]).then_inc(e_r[b], 16)
                run_groups(sp, body)

            @block.gpsimd
            def _(gp):
                def body(tile, n, b, g):
                    at_least(gp, e_o[b], n * 16)
                    gp.wait_ge(e_i[b], n + 1)
                    apart(gp, e_sep)
                    for c in range(2):
                        nc.gpsimd.indirect_dma_start(out=y1[:, b, c, :], out_offset=None, in_=ys_d,
                                                     in_offset=bass.IndirectOffsetOnAxis(ap=idx[:, b, c:c + 1], axis=0)).then_inc(e_y[b], 16)
                run_groups(gp, body)

            @block.vector
            def _(v):
                STT = nc.vector.scalar_tensor_tensor

                def body(tile, n, b, g):
                    v.wait_ge(e_r[b], n * 16 + 16)
                    v.wait_ge(e_y[b], n * 32 + 32)
                    after = 1 if isinstance(tile, int) and tile == 0 else tile + NBUF
                    nc.vector.tensor_copy(idx[:, b:b + 1, :], rows_y[:, bass.ds(after, 1), :]).then_inc(e_i[b], 1)
                    wv = lambda c: wts[:, bass.ds(tile, 1), c]
                    STT(rr[:, b, :], y1[:, b, 0, :], wv(0), rr[:, b, :], ALU.mult, ALU.add).then_inc(e_m, 1)
                    v.wait_ge(e_m, tile + 1)
                    STT(rr[:, b, :], y1[:, b, 1, :], wv(1), rr[:, b, :], ALU.mult, ALU.add).then_inc(e_f, 1)
                nc.vector.tensor_copy(idx[:, 0, :], rows_y[:, 0, :]).then_inc(e_i[0], 1)
                for b in range(1, NBUF):
                    nc.vector.tensor_copy(idx[:, b, :], rows_y[:, 1 + b, :]).then_inc(e_i[b], 1)
                run_groups(v, body)

            @block.scalar
            def _(act):
                def body(tile, n, b, g):
                    act.wait_ge(e_f, tile + 1)
                    if isinstance(tile, int) and tile == 0:
                        act.dma_start(out[:, 0:1, :].rearrange("(o c) t d -> o c (t d)", o=1),
                                      rr[0:1, b, :].rearrange("p (o d) -> p o d", o=1).broadcast_to([1, B, D])).then_inc(e_o[b], 16)
                        return
                    c0 = (b % 2) * (B // 2)
                    t0_ = g * (2 * TC) + (1 + (b // 2) * TC)
                    act.dma_start(out[c0:c0 + B // 2, bass.ds(t0_, TC), :], rr[:, b, :]).then_inc(e_o[b], 16)
                run_groups(act, body)
                for b in range(NBUF):
                    act.wait_ge(e_o[b], 16 * (GR + (b == 0)))


_INS = ["x", "cls_tok", "L0_tok_log_dt", "L0_tok_B_ri", "L0_tok_inv_A_real", "L0_tok_A_imag", "L0_attn_gamma", "L0_attn_beta",
        "L0_attn_W_in", "L0_attn_b_in", "L0_attn_W_out", "L0_attn_b_out", "L0_attn_W_skip", "L0_attn_b_skip", "L0_ffn_gate_w",
        "L0_ffn_w_gate", "L0_ffn_w_up", "L0_ffn_w_down", "L0_ffn_sw_gate", "L0_ffn_sw_up", "L0_ffn_sw_down"]


def kernel(**inputs):
    import numpy as _np
    import concourse.bacc as _bacc
    from concourse import mybir as _mybir
    from concourse.bass_utils import run_bass_kernel_spmd as _run

    nc = _bacc.Bacc("TRN2", target_bir_lowering=False, num_devices=1)
    arrays, args = {}, []
    for name in _INS:
        a = _np.ascontiguousarray(inputs[name])
        arrays["in_" + name] = a
        args.append(nc.dram_tensor("in_" + name, a.shape, _mybir.dt.from_np(a.dtype), kind="ExternalInput").ap())
    out = nc.dram_tensor("out", (B, T + 1, D), F32, kind="ExternalOutput").ap()
    vit_tower(nc, *args, out)
    r = _run(nc, [arrays], core_ids=[0])
    return r.results[0]["out"]
```

```python
import concourse.bass as bass
from concourse import mybir
from contextlib import ExitStack

F32 = mybir.dt.float32
F16 = mybir.dt.float16
I32 = mybir.dt.int32
ALU = mybir.AluOpType
ACT = mybir.ActivationFunctionType
AX = mybir.AxisListType

P = 128
B, T, N, D = 16, 256, 64, 512
S = 128
E, H = 8, 352
HS = 2 * H
EPS = 1e-5
KD = D // P
J = T // 2
NB = 8
NA = D // NB
TC = 16
JC = TC // 2
NCH = T // TC
TOK = B * TC
TILES = 1 + 2 * NCH
SHM = 5
SHT = HS - SHM * P
KH = (H + P - 1) // P
HK = [min(P, H - i * P) for i in range(KH)]
SW, SX, SY = 64.0, 256.0, 4.0
SXW = 1.0 / (SX * SW)
CAP = ((B * T + 1 + P - 1) // P + 1) * P
NSLOT = (2 * (B * T + 1) + E * (P - 1)) // P + 1
NSLOT += NSLOT % 2
ZERO = E * CAP
DUMP = ZERO + P
NR = DUMP + 2 * P
UG = (KD // 2) * 2 * 2 * H
UD = KH * 2 * (D // 2)
UW = UG + UD
NBUF = 4
PER_POOL, PER_DVE = 13, 51


def at_least(eng, sem, value):
    if isinstance(value, int) and value <= 0:
        return
    eng.wait_ge(sem, value)


def apart(eng, sem):
    eng.sem_inc(sem, 1)


class Chain:

    def __init__(self, eng, sem):
        self.eng, self.sem, self.n = eng, sem, 0
        self.loop = None

    def value(self):
        if self.loop is None:
            return self.n
        i, first, start, per = self.loop
        return (i - first) * per + self.n

    def do(self, ins):
        ins.then_inc(self.sem, 1)
        self.n += 1

    def sync(self):
        self.eng.wait_ge(self.sem, self.value())

    def link(self, ins):
        self.do(ins)
        self.sync()

    def enter(self, i, first, per):
        self.loop = (i, first, self.n, per)

    def leave(self, trips):
        i, first, start, per = self.loop
        assert self.n - start == per, ("instructions in the loop", self.n - start)
        self.n = start + per * trips
        self.loop = None


def vit_tower(nc, x, cls_tok, log_dt, b_ri, inv_a_real, a_imag, gamma, beta, w_in, b_in, w_out, b_out,
              w_skip, b_skip, gate_w, w_gate, w_up, w_down, sw_gate, sw_up, sw_down, out):
    top = ExitStack()

    def sem(name):
        return top.enter_context(nc.semaphore(name))

    def sb_in(stack):
        return lambda name, shape, dt: stack.enter_context(nc.sbuf_tensor(name, shape, dt))

    hs_d = nc.dram_tensor("h_tok", [NCH, TOK, D], F32).ap()
    xs_d = nc.dram_tensor("x_slots", [NR, 2 * D], F16).ap()
    ys_d = nc.dram_tensor("y_slots", [NSLOT * P, D], F32).ap()
    rs_d = nc.dram_tensor("resid", [TILES * P, D], F32).ap()
    w16_d = nc.dram_tensor("w_halves", [2 * E, P, UW], F16).ap()

    with top:
        keep = sb_in(top)
        psum = [top.enter_context(nc.psum_tensor(f"bank{i}", [P, D], F32)) for i in range(8)]

        slots = keep("slots", [P, TILES, 2], F32)
        rows_y = keep("rows_y", [P, TILES + NBUF, 2], I32)
        logits = keep("logits", [P, TILES, E], F32)
        top_l = keep("top_l", [P, TILES, 2], F32)
        run = keep("run", [P, E], F32)
        ident16 = keep("ident16", [P, P], F16)
        pcol = keep("pcol", [P, 1], F32)
        zrow = keep("zrow", [P, 2 * D], F16)
        rev = keep("rev", [P, 2, E], F32)

        phase1 = ExitStack()
        sb = sb_in(phase1)
        wsgu = sb("wsgu", [P, KD, 2, 2 * HS], F16)
        wsd = sb("wsd", [P, SHM + 1, 2, D], F16)
        win = sb("win", [P, KD, 2, 3 * S], F16)
        wout = sb("wout", [P, 2, D], F16)
        wskip = sb("wskip", [P, KD, 2, D], F16)
        gw = sb("gw", [P, KD, 2, E], F16)
        brow = sb("brow", [1, 2, D], F16)
        ones_row = sb("ones_row", [1, P], F16)
        tri = sb("tri", [P, P], F16)
        ones16 = sb("ones16", [P, P], F16)
        cb = sb("cb", [P, 3], F32)
        cbh = sb("cbh", [P, 1], F32)
        mask0 = sb("mask0", [P, 1], F32)
        dump_s = sb("dump_s", [P, 2], F32)
        cT = sb("cT", [P, 2, B, J], F32)
        pe_ = sb("pe", [P, 2, NB, J], F32)
        pg = sb("pg", [P, 2, NB, J], F32)
        ph = sb("ph", [P, 2, NB, J], F32)

        with ExitStack() as ph0:
            t0 = sb_in(ph0)
            xj = t0("xj", [P, B, 2 * N, 2], F32)
            cj = t0("cj", [P, 2, B, 2 * N], F32)
            ctmp = t0("ctmp", [P, 2, B // 2, 2 * N], F32)
            itmp = t0("itmp", [P, 2, B // 2, 2 * N], F32)
            bj = t0("bj", [P, 2 * N, 2], F32)
            aj = t0("aj", [P, 2, 2 * N], F32)
            dtj = t0("dtj", [P, 2], F32)
            pw_ = t0("pw_", [P, 24, 2 * N], F32)
            dj = t0("dj", [P, 2, 2 * N], F32)
            mtmp = t0("mtmp", [P, 2, 2, 4 * J], F32)
            sq = t0("sq", [P, 4, 2, J], F32)
            identf = t0("identf", [P, P], F32)
            gam = t0("gam", [P, KD], F32)
            gams = t0("gams", [P, KD], F32)
            bet = t0("bet", [P, KD], F32)
            bin_ = t0("bin_", [P, 3], F32)
            bo = t0("bo", [1, 3, D], F32)
            st = [t0(f"st{i}", [P, 4, D], F32) for i in range(2)]
            st += [xj[:, h * 8:(h + 1) * 8].rearrange("p c (u n) r -> p (c u n r)", u=2).rearrange("p (k n) -> p k n", n=D)
                   for h in range(2)]
            io = t0("io", [P, 2, E], I32)
            pi = t0("pi", [P, 1], I32)

            p_in = sem("p_in")
            p_x = sem("p_x")
            st_in = [sem(f"st_in{b}") for b in range(4)]
            st_sc = sem("st_sc")
            st_hi = sem("st_hi")
            st_lo = sem("st_lo")
            st_lv = sem("st_lv")
            p_act = sem("p_act")
            p_gp = sem("p_gp")
            p_v = sem("p_v")
            p_ct = sem("p_ct")
            p_tp = sem("p_tp")
            p_te = sem("p_te")
            p_cb = sem("p_cb")
            p_z = sem("p_z")
            p_f = sem("p_f")
            p_cf = sem("p_cf")

            def rows(w):
                return w.rearrange("(k p) n -> p k n", p=P)

            jobs = [("win", rows(w_in), 3 * S)]
            jobs += [("wskip", rows(w_skip), D)]
            jobs += [("wout", w_out.rearrange("(k p) n -> p k n", p=P), D)]
            jobs += [("gw", rows(gate_w), E)]
            for kind, w in (("g", sw_gate), ("u", sw_up)):
                r = rows(w)
                jobs += [(kind + "0", r[:, :, 0:SHM * P // 2], SHM * P // 2), (kind + "1", r[:, :, SHM * P // 2:SHM * P], SHM * P // 2),
                         (kind + "t", r[:, :, SHM * P:HS], SHT)]
            jobs += [("d0", sw_down[0:4 * P, :].rearrange("(k p) n -> p k n", p=P), D)]
            jobs += [("d1", sw_down[4 * P:5 * P, :].rearrange("(k p) n -> p k n", p=P), D)]
            jobs += [("d2", sw_down[5 * P:HS, :].rearrange("(k p) n -> p k n", k=1), D)]

            def half(kind, h):
                if kind == "win":
                    return win[:, :, h, :]
                if kind == "wskip":
                    return wskip[:, :, h, :]
                if kind == "wout":
                    return wout[:, h:h + 1, :]
                if kind == "gw":
                    return gw[:, :, h, :]
                if kind == "d0":
                    return wsd[:, 0:4, h, :]
                if kind == "d1":
                    return wsd[:, 4:5, h, :]
                if kind == "d2":
                    return wsd[SHT:2 * SHT, 5:6, h, :]
                c0 = 0 if kind[0] == "g" else SHM * P
                if kind[1] == "t":
                    c0, n = 2 * SHM * P + (0 if kind[0] == "g" else SHT), SHT
                else:
                    n = SHM * P // 2
                    c0 += int(kind[1]) * n
                return wsgu[:, :, h, c0:c0 + n]

            def staged(i):
                kind, src, n = jobs[i]
                k = src.shape[1]
                if kind == "d2":
                    return st[i % 4][SHT:2 * SHT, 0:1, 0:n]
                return st[i % 4][:, 0:k, 0:n]

            on_pool = lambda i: i < len(jobs) - 4

            block = ph0.enter_context(nc.Block())

            @block.sync
            def _(sp):
                sp.dma_start(dtj[:], log_dt.rearrange("(j t) -> j t", t=2)).then_inc(p_in, 16)
                sp.dma_start(aj[:, 0, :], inv_a_real.rearrange("(j t) n -> j (t n)", t=2)).then_inc(p_in, 16)
                sp.dma_start(aj[:, 1, :], a_imag.rearrange("(j t) n -> j (t n)", t=2)).then_inc(p_in, 16)
                sp.dma_start(bj[:], b_ri.rearrange("(j t) n r -> j (t n) r", t=2)).then_inc(p_in, 16)
                sp.dma_start(gam[:], gamma.rearrange("(k p) -> p k", p=P), allow_slow_non_contiguous=True).then_inc(p_in, 16)
                sp.dma_start(bet[:], beta.rearrange("(k p) -> p k", p=P), allow_slow_non_contiguous=True).then_inc(p_in, 16)
                sp.dma_start(bin_[:], b_in.rearrange("(k p) -> p k", p=P), allow_slow_non_contiguous=True).then_inc(p_in, 16)
                sp.dma_start(bo[:, 0, :], b_out.rearrange("(a n) -> a n", a=1)).then_inc(p_in, 16)
                sp.dma_start(bo[:, 1, :], b_skip.rearrange("(a n) -> a n", a=1)).then_inc(p_in, 16)
                sp.dma_start(xj[:].rearrange("j c n r -> j c (n r)"),
                             x.rearrange("c (j t) n r -> j c (t n r)", t=2)).then_inc(p_x, 16)
                for i, (kind, src, n) in enumerate(jobs):
                    at_least(sp, st_lo, i - 3)
                    if i == 2:
                        sp.wait_ge(p_ct, 2)
                        sp.wait_ge(p_cf, 4)
                    sp.dma_start(staged(i), src).then_inc(st_in[i % 4], 16)
                sp.wait_ge(p_gp, 5)
                sp.dma_start(xs_d[ZERO:ZERO + P, :], zrow[:]).then_inc(p_z, 16)
                sp.wait_ge(p_z, 16)

            @block.gpsimd
            def _(gp):
                nc.gpsimd.memset(ident16[:], 0.0).then_inc(p_gp, 1)
                nc.gpsimd.memset(identf[:], 0.0).then_inc(p_gp, 1)
                nc.gpsimd.memset(tri[:], 1.0).then_inc(p_gp, 1)
                nc.gpsimd.memset(ones16[:], 1.0).then_inc(p_gp, 1)
                nc.gpsimd.memset(zrow[:], 0.0).then_inc(p_gp, 1)
                nc.gpsimd.memset(ones_row[:], 1.0).then_inc(p_gp, 1)
                gp.wait_ge(p_gp, 6)
                for m in (ident16, identf):
                    nc.gpsimd.affine_select(out=m[:], in_=m[:], compare_op=ALU.not_equal, fill=1.0, base=0,
                                            pattern=[[-1, P]], channel_multiplier=1).then_inc(p_gp, 1)
                nc.gpsimd.affine_select(out=tri[:], in_=tri[:], compare_op=ALU.is_gt, fill=0.0, base=0,
                                        pattern=[[1, P]], channel_multiplier=-1).then_inc(p_gp, 1)
                nc.gpsimd.iota(io[:], pattern=[[0, 2], [1, E]], base=0, channel_multiplier=0).then_inc(p_gp, 1)
                nc.gpsimd.iota(pi[:], pattern=[[0, 1]], base=0, channel_multiplier=1).then_inc(p_gp, 1)
                TT = nc.gpsimd.tensor_tensor
                gp.wait_ge(p_x, 16)
                gp.wait_ge(p_f, 1)
                for h in range(2):
                    c = slice(h * (B // 2), (h + 1) * (B // 2))
                    f = lambda i: pw_[:, i:i + 1, :].broadcast_to([P, B // 2, 2 * N])
                    at_least(gp, p_cf, 2 * h)
                    TT(itmp[:, 0], xj[:, c, :, 0], f(14), ALU.mult)
                    TT(itmp[:, 1], xj[:, c, :, 1], f(12), ALU.mult).then_inc(p_cf, 1)
                    gp.wait_ge(p_cf, 2 * h + 1)
                    TT(cj[:, 1, c], itmp[:, 0], itmp[:, 1], ALU.add).then_inc(p_cf, 1)
                for i, (kind, src, n) in enumerate(jobs):
                    if on_pool(i):
                        gp.wait_ge(st_hi, i + 1)
                        TT(half(kind, 1), staged(i), half(kind, 0), ALU.subtract).then_inc(st_lo, 1)

            @block.scalar
            def _(act):
                act.wait_ge(p_in, 9 * 16)
                nc.scalar.activation(pw_[:, 0, 0:2], dtj[:], ACT.Exp).then_inc(p_act, 1)
                nc.scalar.activation(pw_[:, 1, :], aj[:, 0, :], ACT.Exp).then_inc(p_act, 1)
                nc.scalar.activation(gams[:], gam[:], ACT.Copy, scale=SW).then_inc(st_sc, 1)
                act.wait_ge(st_sc, 1)

                def scale(i):
                    act.wait_ge(st_in[i % 4], 16 * (i // 4 + 1))
                    if jobs[i][0] == "win":
                        act.wait_ge(p_cb, 1)
                        for k in range(KD):
                            last = nc.scalar.activation(staged(i)[:, k, :], staged(i)[:, k, :], ACT.Copy, scale=gams[:, k:k + 1])
                    else:
                        last = nc.scalar.activation(staged(i), staged(i), ACT.Copy, scale=SW)
                    last.then_inc(st_sc, 1)

                def coefficients(g):
                    r, c0 = g // 4, (g % 4) * 4
                    act.wait_ge(p_tp, g + 2)
                    nc.scalar.activation(cT[:, r, c0:c0 + 4, :].rearrange("p c j -> p (c j)"), psum[1 + g % 6][:],
                                         ACT.Copy).then_inc(p_te, 1)

                scale(0)
                for i, (kind, src, n) in enumerate(jobs):
                    if i + 1 < len(jobs):
                        scale(i + 1)
                    act.wait_ge(st_sc, i + 2)
                    nc.scalar.activation(half(kind, 0), staged(i), ACT.Copy).then_inc(st_hi, 1)
                    if i in (4, 8):
                        for g in range(i - 4, i):
                            coefficients(g)

            @block.tensor
            def _(pe):
                pe.wait_ge(p_gp, 8)
                pe.wait_ge(st_in[0], 16)
                pe.wait_ge(p_in, 9 * 16)
                for m in range(3):
                    for k in range(KD):
                        last = nc.tensor.matmul(psum[7][:, m:m + 1], st[0][:, k, m * S:(m + 1) * S],
                                                bet[:, k:k + 1], start=(k == 0), stop=(k == KD - 1))
                last.then_inc(p_cb, 1)
                pe.wait_ge(p_ct, 1)
                for r in range(2):
                    last = nc.tensor.transpose(psum[0][:, r * J:(r + 1) * J], dj[:, r, :], identf[:])
                last.then_inc(p_tp, 1)
                pe.wait_ge(p_ct, 2)
                for g in range(8):
                    r, c0 = g // 4, (g % 4) * 4
                    if g == 4:
                        pe.wait_ge(p_cf, 4)
                    if g >= 6:
                        pe.wait_ge(p_te, g - 5)
                    for c in range(4):
                        last = nc.tensor.transpose(psum[1 + g % 6][:, c * J:(c + 1) * J],
                                                   cj[:, r, c0 + c, :], identf[:])
                    last.then_inc(p_tp, 1)

            @block.vector
            def _(v):
                ch = Chain(v, p_v)
                link = ch.link
                TT, TS, STT = nc.vector.tensor_tensor, nc.vector.tensor_scalar, nc.vector.scalar_tensor_tensor
                v.wait_ge(p_in, 9 * 16)
                v.wait_ge(p_act, 2)
                w = lambda i: pw_[:, i, :]
                dtb = pw_[:, 0, 0:2].rearrange("p (t o) -> p t o", o=1).broadcast_to([P, 2, N])
                two = lambda ap: ap.rearrange("p (t n) -> p t n", t=2)
                link(TT(two(w(2)), two(w(1)), dtb, ALU.mult))
                link(TS(w(2), w(2), -0.5, None, ALU.mult))
                link(TT(two(w(3)), two(aj[:, 1, :]), dtb, ALU.mult))
                link(TS(w(3), w(3), 0.5, None, ALU.mult))
                link(TS(w(4), w(2), -1.0, 1.0, ALU.mult, ALU.add))
                link(TT(w(5), w(4), w(4), ALU.mult))
                link(TT(w(6), w(3), w(3), ALU.mult))
                link(TT(w(7), w(5), w(6), ALU.add))
                link(nc.vector.reciprocal(w(8), w(7)))
                link(TS(w(9), w(2), 1.0, None, ALU.add))
                link(TT(w(10), w(9), w(4), ALU.mult))
                link(TT(w(10), w(10), w(6), ALU.subtract))
                link(TT(dj[:, 0, :], w(10), w(8), ALU.mult))
                link(TS(w(11), w(3), 2.0, None, ALU.mult))
                v.wait_ge(p_gp, 11)
                TT(dj[:, 1, :], w(11), w(8), ALU.mult).then_inc(p_ct, 1)
                br, bi = bj[:, :, 0], bj[:, :, 1]
                link(TT(w(12), br, w(4), ALU.mult))
                link(TT(w(13), bi, w(3), ALU.mult))
                link(TT(w(12), w(12), w(13), ALU.subtract))
                link(TT(w(14), br, w(3), ALU.mult))
                link(TT(w(15), bi, w(4), ALU.mult))
                link(TT(w(14), w(14), w(15), ALU.add))
                link(TT(two(w(16)), two(w(8)), dtb, ALU.mult))
                link(TS(w(16), w(16), 2.0, None, ALU.mult))
                link(TT(w(12), w(12), w(16), ALU.mult))
                TT(w(14), w(14), w(16), ALU.mult).then_inc(p_f, 1)
                v.wait_ge(p_f, 1)
                v.wait_ge(p_x, 16)
                for h in range(2):
                    c = slice(h * (B // 2), (h + 1) * (B // 2))
                    f = lambda i: pw_[:, i:i + 1, :].broadcast_to([P, B // 2, 2 * N])
                    ch.do(TT(ctmp[:, 0], xj[:, c, :, 0], f(12), ALU.mult))
                    link(TT(ctmp[:, 1], xj[:, c, :, 1], f(14), ALU.mult))
                    ins = TT(cj[:, 0, c], ctmp[:, 0], ctmp[:, 1], ALU.subtract)
                    if h == 0:
                        link(ins)
                    else:
                        ins.then_inc(p_ct, 1)
                link(TS(rev[:], io[:], -1.0, float(E), ALU.mult, ALU.add))
                link(nc.vector.tensor_copy(pcol[:], pi[:]))
                link(TS(mask0[:], pcol[:], 0.0, None, ALU.is_equal))
                link(TS(run[:], io[:, 0, :], float(CAP), None, ALU.mult))
                link(TS(dump_s[:, 0:1], mask0[:], -1.0, 1.0, ALU.mult, ALU.add))
                link(TS(dump_s[:, 1:2], pcol[:], float(DUMP + P), dump_s[:, 0:1], ALU.add, ALU.mult))
                link(TS(dump_s[:, 0:1], pcol[:], float(DUMP), dump_s[:, 0:1], ALU.add, ALU.mult))
                v.wait_ge(p_cb, 1)
                link(TT(cb[:], psum[7][:, 0:3], bin_[:], ALU.add))
                link(TS(cbh[:], cb[:, 0:1], 0.5, None, ALU.mult))
                link(TT(bo[:, 2, :], bo[:, 0, :], bo[:, 1, :], ALU.add))
                link(TS(brow[:, 0, :], bo[:, 2, :], SW * SY, None, ALU.mult))
                link(STT(brow[:, 1, :], bo[:, 2, :], SW * SY, brow[:, 0, :], ALU.mult, ALU.subtract))
                link(nc.vector.memset(rows_y[:, TILES:, :], 0))
                link(nc.vector.memset(pe_[:, 0, 0:1, :], 1.0))
                for tab in (pe_, pg, ph):
                    if tab is not pe_:
                        link(nc.vector.memset(tab[:, 0, 0:1, :], 1.0))
                    link(nc.vector.memset(tab[:, 1, 0:1, :], 0.0))
                v.wait_ge(p_tp, 1)
                for r in range(2):
                    link(nc.vector.tensor_copy(pe_[:, r, 1, :], psum[0][:, r * J:(r + 1) * J]))

                def cmul(dst, a, b, n):
                    m = lambda i: mtmp[:, i].rearrange("p r (n j) -> p r n j", j=J)[:, :, 0:n, :]
                    for r in range(2):
                        w = b[:, r:r + 1].rearrange("p r (o j) -> p r o j", o=1).broadcast_to([P, 2, n, J])
                        (ch.do if r == 0 else link)(TT(m(r), a, w, ALU.mult))
                    ch.do(TT(dst[:, 0], m(0)[:, 0], m(1)[:, 1], ALU.subtract))
                    link(TT(dst[:, 1], m(0)[:, 1], m(1)[:, 0], ALU.add))

                for n, tab in enumerate((pe_, pg, ph)):
                    cmul(sq[:, 0, :, :].rearrange("p r (o j) -> p r o j", o=1), tab[:, 0:2, 1:2, :], tab[:, 0:2, 1, :], 1)
                    cmul(tab[:, 0:2, 2:4, :], tab[:, 0:2, 0:2, :], sq[:, 0], 2)
                    cmul(sq[:, 1, :, :].rearrange("p r (o j) -> p r o j", o=1), sq[:, 0].rearrange("p r (o j) -> p r o j", o=1), sq[:, 0], 1)
                    cmul(tab[:, 0:2, 4:8, :], tab[:, 0:2, 0:4, :], sq[:, 1], 4)
                    if n < 2:
                        cmul((pg, ph)[n][:, 0:2, 1:2, :], sq[:, 1].rearrange("p r (o j) -> p r o j", o=1), sq[:, 1], 1)
                for i, (kind, src, n) in enumerate(jobs):
                    if not on_pool(i):
                        v.wait_ge(st_hi, i + 1)
                        TT(half(kind, 1), staged(i), half(kind, 0), ALU.subtract).then_inc(st_lv, 1)

        hx = sb("hx", [P, 2, D], F32)
        hc = sb("hc", [P, 2, D], F32)
        xf = sb("xf", [P, 2, D], F32)
        x2r = sb("x2r", [P, 2, 2, D], F16)
        x2T = sb("x2T", [P, 2, KD, TOK], F16)
        x3r = sb("x3r", [P, 2, 2, D], F16)
        x3T = sb("x3T", [P, 2, KD, TOK], F16)
        h2 = sb("h2", [P, 2, D], F32)
        r_o = sb("r_o", [P, 2, D], F32)
        stat = sb("stat", [P, 2, 2, 6], F32)
        mv = sb("mv", [P, 2, 2, 2], F32)
        sc = sb("sc", [P, 8, 2], F32)
        pwc = sb("pwc", [P, 2, 2], F32)
        ir = sb("ir", [P, 2], F32)
        th = sb("th", [P, TOK], F32)
        tc = sb("tc", [P, TOK], F32)
        al = sb("al", [P, TOK], F32)
        om = sb("om", [P, TOK], F32)
        bb = sb("bb", [P, TOK], F32)
        hsc = sb("hsc", [P, TOK], F32)
        carry = sb("carry", [P, B], F32)
        fix = sb("fix", [P, B], F32)
        yT = sb("yT", [P, 2, TOK], F16)
        sgs = sb("sgs", [P, 2, TOK], F32)
        gf = sb("gf", [P, 2, TOK], F32)
        gT = sb("gT", [P, SHM + 1, 2, TOK], F16)
        ea = sb("ea", [P, 2, JC, 2, NA], F32)
        et = sb("et", [P, 4, JC, NA], F32)
        pp = sb("pp", [P, 2, JC, NB, B], F32)
        pt = sb("pt", [P, 2, JC, NB, B], F32)
        hst = sb("hst", [P, JC, 2, NA], F32)
        rt = sb("rt", [P, 8, 2, E], F32)
        rm = sb("rm", [P, 8, 2], F32)
        m16 = sb("m16", [P, 2, E], F16)
        oh = sb("oh", [P, 2, 2, E], F32)
        zi = sb("zi", [P, E], I32)
        sl = sb("sl", [P, 2, 2], I32)

        HK2 = KD // 2
        rgu = sb("rgu", [P, 2, HK2, H], F32)
        rdn = sb("rdn", [P, KH, D // 2], F32)
        hgu = sb("hgu", [P, HK2, 2, 2 * H], F16)
        hdn = sb("hdn", [P, KH, 2, D // 2], F16)

        BX = [psum[0], psum[3]]
        BU = [psum[1], psum[2]]
        BD, BS, BY, BG, BB = psum[3], psum[4], psum[5], psum[6], psum[7]

        c_tokp = sem("c_tokp")
        c_tokm = sem("c_tokm")
        c_toke = sem("c_toke")
        c_hst = sem("c_hst")
        c_hx = sem("c_hx")
        c_prom = sem("c_prom")
        c_irc = sem("c_irc")
        c_st2 = sem("c_st2")
        c_pw2 = sem("c_pw2")
        c_xf2 = sem("c_xf2")
        c_hi2 = sem("c_hi2")
        c_lo2 = sem("c_lo2")
        c_t2 = sem("c_t2")
        c_e2 = sem("c_e2")
        c_gt = sem("c_gt")
        c_th = sem("c_th")
        c_yf = sem("c_yf")
        c_yh = sem("c_yh")
        c_yl = sem("c_yl")
        c_out = sem("c_out")
        c_oev = sem("c_oev")
        c_st3 = sem("c_st3")
        c_pw3 = sem("c_pw3")
        c_xf3 = sem("c_xf3")
        c_hi3 = sem("c_hi3")
        c_lo3 = sem("c_lo3")
        c_t3 = sem("c_t3")
        c_e3 = sem("c_e3")
        c_rt = sem("c_rt")
        c_m = sem("c_m")
        c_rk = sem("c_rk")
        c_sl = sem("c_sl")
        c_sca = sem("c_sca")
        c_up = sem("c_up")
        c_sg = sem("c_sg")
        c_gm = sem("c_gm")
        c_gh = sem("c_gh")
        c_gl = sem("c_gl")
        c_dn = sem("c_dn")
        c_dev = sem("c_dev")
        c_ro = sem("c_ro")
        c_sep = sem("c_sep")
        c_wi = sem("c_wi")
        c_ws = sem("c_ws")
        c_wh = sem("c_wh")
        c_wl = sem("c_wl")
        c_wo = sem("c_wo")
        c_v = sem("c_v")
        c_p = sem("c_p")
        c_cst = sem("c_cst")

        tiles = lambda k: 1 if isinstance(k, int) and k == 0 else 2
        cols = lambda k: tiles(k) * P
        LOOP0, LOOP1 = 2, NCH - 2
        LAST = NCH + 1
        clampc = lambda k: k if not isinstance(k, int) else min(k, NCH)

        def iterate(eng, body, chain=None, per=None):
            body(-1)
            for k in range(LOOP0):
                body(k)
            with eng.Fori(LOOP0, LOOP1) as k:
                if chain is not None:
                    chain.enter(k, LOOP0, per)
                body(k)
            if chain is not None:
                chain.leave(LOOP1 - LOOP0)
            for k in range(LOOP1, LAST + 1):
                body(k)

        has = lambda k: not isinstance(k, int) or 0 <= k <= NCH
        htok = lambda k: not isinstance(k, int) or 1 <= k <= NCH
        rows_of = lambda k: (0 if isinstance(k, int) and k == 0 else k * 2 - 1)

        with nc.Block() as block:

            @block.sync
            def _(sp):
                w_g = w_gate.rearrange("e (s k p) n -> (e s) p k n", s=2, p=P)
                w_u = w_up.rearrange("e (s k p) n -> (e s) p k n", s=2, p=P)
                one = lambda ap, u: ap[bass.ds(u, 1)]

                def load_unit(u):
                    for g, w in enumerate((w_g, w_u)):
                        sp.dma_start(rgu[:, g], one(w, u).rearrange("u p k n -> (u p) k n")).then_inc(c_wi, 16)
                    e, c = u // 2, u % 2 * (D // 2)
                    src = w_down[bass.ds(e, 1), :, bass.ds(c, D // 2)].rearrange("e h d -> (e h) d")
                    sp.dma_start(rdn[:, 0:2, :], src[0:2 * P].rearrange("(k p) d -> p k d", p=P)).then_inc(c_wi, 16)
                    sp.dma_start(rdn[0:HK[2], 2, :], src[2 * P:H]).then_inc(c_wi, 16)

                def store_unit(u):
                    dst = one(w16_d, u).rearrange("u p n -> (u p) n")
                    sp.dma_start(dst[:, 0:UG], hgu[:].rearrange("p k h n -> p (k h n)")).then_inc(c_wo, 16)
                    sp.dma_start(dst[:, UG:UW], hdn[:].rearrange("p k h n -> p (k h n)")).then_inc(c_wo, 16)

                def body(k):
                    if htok(k + 1):
                        n = k + 1
                        sp.wait_ge(c_hst, n * NB * 16)
                        at_least(sp, c_prom, n)
                        sp.wait_ge(c_lo2, n)
                        src = hs_d[bass.ds(n - 1, 1)].rearrange("q (i p) d -> p (q i) d", p=P)
                        sp.dma_start(hx[:], src).then_inc(c_hx, 16)
                    elif k + 1 == 0:
                        sp.dma_start(hx[:, 0, :], cls_tok.rearrange("a b d -> (a b) d").broadcast_to([P, D])).then_inc(c_hx, 16)
                    if htok(k - 1):
                        sp.wait_ge(c_wl, k - 1)
                        store_unit(k - 2)
                    if htok(k):
                        load_unit(k - 1)
                    if has(k - 1):
                        n = k - 1
                        sp.wait_ge(c_dev, (n + 1) * 2)
                        r0 = rows_of(n)
                        dst = rs_d[bass.ds(r0 * P, tiles(n) * P)].rearrange("(i p) d -> p i d", p=P)
                        sp.dma_start(dst, r_o[:, 0:tiles(n), :]).then_inc(c_ro, 16)
                    if htok(k + 2):
                        n = k + 2
                        sp.wait_ge(c_toke, n * 2)
                        dst = hs_d[bass.ds(n - 1, 1)].rearrange("q (c t) (b a) -> b (q c) t a", t=TC, a=NA)
                        for b in range(NB):
                            sp.dma_start(dst[b], hst[b * B:(b + 1) * B].rearrange("c j t a -> c (j t) a")).then_inc(c_hst, 16)

                iterate(sp, body)
                sp.wait_ge(c_ro, 16 * (NCH + 1))
                sp.wait_ge(c_wo, 32 * NCH)

            @block.gpsimd
            def _(gp):
                ch = Chain(gp, c_p)
                gp.wait_ge(c_cst, 1)

                def link(ins):
                    ch.link(ins)
                    apart(gp, c_sep)

                TT, TS = nc.gpsimd.tensor_tensor, nc.gpsimd.tensor_scalar
                link(nc.gpsimd.memset(pwc[:, 0, :], -0.5))
                link(nc.gpsimd.memset(pwc[:, 1, :], 0.5))

                def body(k):
                    if has(k + 1):
                        n = k + 1
                        gp.wait_ge(c_st2, n + 1)
                        at_least(gp, c_xf2, n)
                        at_least(gp, c_prom, n)
                        apart(gp, c_sep)
                        link(TS(sc[:, 0, :], mv[:, 0, :, 1], EPS, None, ALU.add))
                        link(TT(sc[:, 1, :], sc[:, 0, :], pwc[:, 0, :], ALU.pow))
                        link(TT(sc[:, 2, :], sc[:, 1, :], sc[:, 1, :], ALU.mult))
                        link(TT(sc[:, 2, :], sc[:, 2, :], mv[:, 0, :, 1], ALU.mult))
                        link(TS(sc[:, 2, :], sc[:, 2, :], EPS, None, ALU.add))
                        link(TT(sc[:, 3, :], sc[:, 2, :], pwc[:, 0, :], ALU.pow))
                        link(TT(sc[:, 4, :], sc[:, 2, :], pwc[:, 1, :], ALU.pow))
                        link(TS(sc[:, 4, :], sc[:, 4, :], SXW, None, ALU.mult))
                        link(TT(sc[:, 3, :], sc[:, 3, :], sc[:, 1, :], ALU.mult))
                        TS(sc[:, 3, :], sc[:, 3, :], SX, None, ALU.mult).then_inc(c_pw2, 1)
                    if has(k - 1):
                        n = k - 1
                        gp.wait_ge(c_sl, n + 1)
                        gp.wait_ge(c_hi3, n * 2 + 2)
                        gp.wait_ge(c_lo3, n * 2 + 2)
                        apart(gp, c_sep)
                        for i in range(tiles(n)):
                            for c in range(2):
                                nc.gpsimd.indirect_dma_start(
                                    out=xs_d, out_offset=bass.IndirectOffsetOnAxis(ap=sl[:, i, c:c + 1], axis=0),
                                    in_=x3r[:, i].rearrange("p h d -> p (h d)"), in_offset=None,
                                ).then_inc(c_sca, 32 // tiles(n))
                    if has(k):
                        n, nt = k, tiles(k)
                        for i in range(nt):
                            gp.wait_ge(c_st3, n * 2 + (i + 1) * 2 // nt)
                            at_least(gp, c_xf3, n * 2)
                            apart(gp, c_sep)
                            link(TS(sc[:, 5, i:i + 1], mv[:, 1, i, 1:2], EPS, None, ALU.add))
                            link(TT(sc[:, 6, i:i + 1], sc[:, 5, i:i + 1], pwc[:, 0, 0:1], ALU.pow))
                            TS(sc[:, 6, i:i + 1], sc[:, 6, i:i + 1], SX, None, ALU.mult).then_inc(c_pw3, 2 // nt)

                    if htok(k):
                        gp.wait_ge(c_wh, k)
                        for g in range(2):
                            TT(hgu[:, :, 1, g * H:(g + 1) * H], rgu[:, g], hgu[:, :, 0, g * H:(g + 1) * H], ALU.subtract)
                        TT(hdn[:, 0:2, 1, :], rdn[:, 0:2, :], hdn[:, 0:2, 0, :], ALU.subtract)
                        TT(hdn[0:HK[2], 2, 1, :], rdn[0:HK[2], 2, :], hdn[0:HK[2], 2, 0, :], ALU.subtract).then_inc(c_wl, 1)

                iterate(gp, body, ch, PER_POOL)
                gp.wait_ge(c_cst, 3)
                for e in range(E):
                    nc.gpsimd.indirect_dma_start(
                        out=xs_d, out_offset=bass.IndirectOffsetOnAxis(ap=zi[:, e:e + 1], axis=0),
                        in_=zrow[:], in_offset=None).then_inc(c_sca, 16)
                gp.wait_ge(c_sca, 64 * (NCH + 1) + 16 * E)

            @block.tensor
            def _(pe):
                MM = nc.tensor.matmul

                def split3(dst, stat_of, mov_of, steps):
                    last = None
                    parts = [(0, 0), (0, 1), (1, 0)]
                    for s_, step in enumerate(steps):
                        for a, b in parts:
                            last = MM(dst, stat_of(step, a), mov_of(step, b),
                                      start=(s_ == 0 and a + b == 0), stop=(s_ == len(steps) - 1 and a == 1))
                    return last

                def transposes(bank, rows):
                    for h in range(2):
                        for c in range(KD):
                            last = nc.tensor.transpose(bank[:].bitcast(F16)[:, (h * KD + c) * P:(h * KD + c + 1) * P],
                                                       rows[:, h, c * P:(c + 1) * P], ident16[:])
                    return last

                def features(k, half):
                    n = k + 2
                    pe.wait_ge(c_tokp, n)
                    if not isinstance(k, int) or k >= 1:
                        pe.wait_ge(c_gm, k * 6)
                    for j in range(4 * half, 4 * half + 4):
                        o = j % 4 * 2 * NA
                        for f in range(2):
                            last = MM(BU[half][:, o:o + 2 * NA], pp[:, f, j].rearrange("p b c -> p (b c)"),
                                      ea[:, f, j].rearrange("p t a -> p (t a)"), start=(f == 0), stop=(f == 1))
                    last.then_inc(c_tokm, 1)

                def rows3(n, i):
                    done = n * 2 + (2 if tiles(n) == 1 else i + 1)
                    pe.wait_ge(c_hi3, done)
                    pe.wait_ge(c_lo3, done)
                    if i == 1 and has(n - 1):
                        pe.wait_ge(c_dev, n * 2)
                    if has(n + 1):
                        pe.wait_ge(c_e2, (n + 2) * 2)
                    transposes(BX[i], x3r[:, i]).then_inc(c_t3, 2 // tiles(n))

                def body(k):
                    if has(k - 1):
                        n, w = k - 1, cols(k - 1)
                        pe.wait_ge(c_e3, (n + 1) * 2)
                        at_least(pe, c_toke, clampc(k + 1) * 2)
                        for m in range(SHM + 1):
                            at_least(pe, c_gm, n * 6 + m - 1)
                            bank = BU[m % 2]
                            if m < SHM:
                                for g in range(2):
                                    c0 = g * SHM * P + m * P
                                    last = split3(bank[:, g * TOK:g * TOK + w], lambda s_, a: wsgu[:, s_, a, c0:c0 + P],
                                                  lambda s_, b: x3T[:, b, s_, 0:w], range(KD))
                            else:
                                last = split3(bank[:, 0:w], lambda s_, a: wsgu[:, s_, a, 2 * SHM * P:2 * HS],
                                              lambda s_, b: x3T[:, b, s_, 0:w], range(KD))
                            last.then_inc(c_up, 1)
                            if m == 3:
                                pe.wait_ge(c_m, n + 1)
                                MM(BS[:, 256:256 + 2 * E], tri[:], m16[:].rearrange("p i e -> p (i e)"), start=True, stop=True)
                                MM(BS[:, 288:288 + 2 * E], ones16[:], m16[:].rearrange("p i e -> p (i e)"),
                                   start=True, stop=True).then_inc(c_rk, 1)
                    def project(i):
                        n = k
                        if i == 0:
                            pe.wait_ge(c_yh, n + 1)
                            pe.wait_ge(c_yl, n + 1)
                            at_least(pe, c_sl, n)
                        at_least(pe, c_oev, n * 2 + i)
                        t = slice(i * P, (i + 1) * P)
                        split3(BS[:], lambda s_, a: x2T[:, a, s_, t], lambda s_, b: wskip[:, s_, b, :], range(KD))
                        MM(BY[:], yT[:, 0, t], wout[:, 0, :], start=True, stop=False)
                        MM(BY[:], yT[:, 0, t], wout[:, 1, :], start=False, stop=False)
                        MM(BY[:], yT[:, 1, t], wout[:, 0, :], start=False, stop=False)
                        MM(BY[:], ones_row[:], brow[:, 0, :], start=False, stop=False)
                        MM(BY[:], ones_row[:], brow[:, 1, :], start=False, stop=True).then_inc(c_out, 2 // tiles(n))

                    def shared_down(i):
                        n = k - 1
                        if i == 0:
                            pe.wait_ge(c_gl, k * 6)
                        at_least(pe, c_dev, n * 2 + i)
                        t = slice(i * P, (i + 1) * P)
                        for m in range(SHM + 1):
                            p0 = 0 if m < SHM else SHT
                            for a, b in ((0, 0), (0, 1), (1, 0)):
                                last = MM(BD[:], gT[p0:P, m, a, t], wsd[p0:P, m, b, :], start=(m == 0 and a + b == 0),
                                          stop=(m == SHM and a == 1))
                        last.then_inc(c_dn, 2 // tiles(n))

                    if has(k):
                        project(0)
                    if has(k - 1):
                        shared_down(0)
                    if has(k + 1):
                        n = k + 1
                        pe.wait_ge(c_hi2, n + 1)
                        pe.wait_ge(c_lo2, n + 1)
                        at_least(pe, c_e3, n * 2 - 2)
                        at_least(pe, c_th, n)
                        for q in range(tiles(n)):
                            transposes((psum[0], BG)[q], x2r[:, q]).then_inc(c_t2, 2 // tiles(n))
                    if has(k - 1) and tiles(k - 1) == 2:
                        shared_down(1)
                    if has(k) and tiles(k) == 2:
                        project(1)
                    if htok(k + 2):
                        features(k, 0)
                        features(k, 1)
                    if has(k):
                        rows3(k, 0)
                    for m in range(3):
                        if has(k + 1):
                            n, w = k + 1, cols(k + 1)
                            if m == 0:
                                pe.wait_ge(c_e2, (n + 1) * 2)
                            dst = (BG[:, 0:w], BB[:, 0:w], BG[:, TOK:TOK + w])[m]
                            last = split3(dst, lambda s_, a: win[:, s_, a, m * S:(m + 1) * S],
                                          lambda s_, b: x2T[:, b, s_, 0:w], range(KD))
                            if m == 2:
                                last.then_inc(c_gt, 1)
                        if m == 1 and has(k) and tiles(k) == 2:
                            rows3(k, 1)
                    if has(k):
                        n = k
                        pe.wait_ge(c_e3, (n + 1) * 2)
                        for i in range(tiles(n)):
                            t = slice(i * P, (i + 1) * P)
                            last = split3(BS[:, i * E:(i + 1) * E], lambda s_, a: x3T[:, a, s_, t],
                                          lambda s_, b: gw[:, s_, b, :], range(KD))
                        last.then_inc(c_rt, 1)

                pe.wait_ge(c_cst, 2)
                iterate(pe, body)

            @block.scalar
            def _(act):
                A = nc.scalar.activation

                def rows_hi(n, i):
                    nt = tiles(n)
                    act.wait_ge(c_xf3, n * 2 + (i + 1) * 2 // nt)
                    if i == 0:
                        at_least(act, c_sca, n * 64)
                    A(x3r[:, i, 0, :], xf[:, i, :], ACT.Copy).then_inc(c_hi3, 2 // nt)

                def tok_out(n, half):
                    act.wait_ge(c_tokm, n * 2 - 1 + half)
                    A(hst[:, half * 4:half * 4 + 4].rearrange("p j t a -> p (j t a)"), BU[half][:], ACT.Copy).then_inc(c_toke, 1)

                def silu(n, m):
                    w = cols(n)
                    act.wait_ge(c_up, n * 6 + m + 1)
                    at_least(act, c_gm, n * 6 + m - 1)
                    p1 = P if m < SHM else SHT
                    A(sgs[P - p1:P, m % 2, 0:w], BU[m % 2][0:p1, 0:w], ACT.Silu, scale=SXW).then_inc(c_sg, 1)

                def ghigh(n, m):
                    w, p0 = cols(n), (0 if m < SHM else SHT)
                    act.wait_ge(c_gm, n * 6 + m + 1)
                    at_least(act, c_dn, n * 2)
                    A(gT[p0:P, m, 0, 0:w], gf[p0:P, m % 2, 0:w], ACT.Copy).then_inc(c_gh, 1)

                def body(k):
                    if has(k - 1):
                        silu(k - 1, 0)
                    if has(k):
                        w = cols(k)
                        act.wait_ge(c_yf, k + 1)
                        at_least(act, c_out, k * 2)
                        A(yT[:, 0, 0:w], hsc[:, 0:w], ACT.Copy).then_inc(c_yh, 1)
                    if has(k - 1):
                        silu(k - 1, 1)
                    if has(k):
                        n, nt = k, tiles(k)
                        act.wait_ge(c_hx, (n + 1) * 16)
                        act.wait_ge(c_pw2, n + 1)
                        at_least(act, c_oev, n * 2)
                        A(ir[:], sc[:, 4, :], ACT.Copy).then_inc(c_irc, 1)
                        A(hc[:, 0:nt, :], hx[:, 0:nt, :], ACT.Copy).then_inc(c_prom, 1)
                    if has(k - 1):
                        n = k - 1
                        ghigh(n, 0)
                        for m in range(2, SHM + 1):
                            silu(n, m)
                            ghigh(n, m - 1)
                        ghigh(n, SHM)
                    if has(k + 1):
                        n, nt = k + 1, tiles(k + 1)
                        act.wait_ge(c_xf2, n + 1)
                        at_least(act, c_t2, n * 2)
                        A(x2r[:, 0:nt, 0, :], xf[:, 0:nt, :], ACT.Copy).then_inc(c_hi2, 1)
                    if has(k):
                        rows_hi(k, 0)
                    if has(k + 1):
                        n, nt = k + 1, tiles(k + 1)
                        at_least(act, c_out, (k + 1) * 2)
                        for i in range(nt):
                            act.wait_ge(c_t2, n * 2 + (i + 1) * 2 // nt)
                            A(x2T[:, :, :, i * P:(i + 1) * P].rearrange("p h k t -> p (h k) t"),
                              (psum[0], BG)[i][:].bitcast(F16).rearrange("p (c t) -> p c t", t=P), ACT.Copy).then_inc(c_e2, 2 // nt)
                    def rows_t(i):
                        nt = tiles(k)
                        act.wait_ge(c_t3, k * 2 + (i + 1) * 2 // nt)
                        A(x3T[:, :, :, i * P:(i + 1) * P].rearrange("p h k t -> p (h k) t"),
                          BX[i][:].bitcast(F16).rearrange("p (c t) -> p c t", t=P), ACT.Copy).then_inc(c_e3, 2 // nt)

                    if htok(k + 2):
                        at_least(act, c_hst, (k + 1) * NB * 16)
                        tok_out(k + 2, 0)
                        tok_out(k + 2, 1)
                    if has(k):
                        rows_t(0)
                    if has(k) and tiles(k) == 2:
                        rows_hi(k, 1)
                    if htok(k):
                        act.wait_ge(c_wi, k * 64)
                        at_least(act, c_wo, k * 32 - 32)
                        A(rgu[:], rgu[:], ACT.Copy, scale=SW)
                        A(rdn[:, 0:2, :], rdn[:, 0:2, :], ACT.Copy, scale=SW)
                        A(rdn[0:HK[2], 2, :], rdn[0:HK[2], 2, :], ACT.Copy, scale=SW).then_inc(c_ws, 1)
                    if has(k) and tiles(k) == 2:
                        rows_t(1)
                    if has(k + 1):
                        n, w = k + 1, cols(k + 1)
                        act.wait_ge(c_gt, n + 1)
                        at_least(act, c_yf, n)
                        A(th[:, 0:w], BG[:, 0:w], ACT.Tanh, bias=cbh[:, 0:1], scale=0.5 * SXW)
                        A(tc[:, 0:w], BG[:, TOK:TOK + w], ACT.Tanh, bias=cb[:, 2:3], scale=SXW).then_inc(c_th, 1)
                    if htok(k):
                        act.wait_ge(c_ws, k)
                        for g in range(2):
                            A(hgu[:, :, 0, g * H:(g + 1) * H], rgu[:, g], ACT.Copy)
                        A(hdn[:, 0:2, 0, :], rdn[:, 0:2, :], ACT.Copy)
                        A(hdn[0:HK[2], 2, 0, :], rdn[0:HK[2], 2, :], ACT.Copy).then_inc(c_wh, 1)

                act.wait_ge(c_cst, 2)
                iterate(act, body)

            @block.vector
            def _(v):
                ch = Chain(v, c_v)
                link = ch.link
                TT, TS, STT = nc.vector.tensor_tensor, nc.vector.tensor_scalar, nc.vector.scalar_tensor_tensor
                RED = nc.vector.tensor_reduce

                def tok_e(n, part):
                    j = bass.ds((n - 1) * JC, JC)
                    shape = [P, JC, NB, NB]
                    gq = lambda r: pg[:, r, :, j].rearrange("p q (j o) -> p j q o", o=1).broadcast_to(shape)
                    er = lambda r: pe_[:, r, :, j].rearrange("p (o r) j -> p j o r", o=1).broadcast_to(shape)
                    o = lambda t: t.rearrange("p j (q r) -> p j q r", r=NB)
                    if part < 4:
                        ins = TT(o(et[:, part]), gq((0, 1, 0, 1)[part]), er((0, 1, 1, 0)[part]), ALU.mult)
                        if part < 3:
                            ch.do(ins)
                        else:
                            link(ins)
                    else:
                        at_least(v, c_tokm, (n - 1) * 2)
                        for t in range(2):
                            q = slice(t * N, (t + 1) * N)
                            ch.do(TT(ea[q, 0, :, t, :], et[q, 0], et[q, 1], ALU.subtract))
                            ch.do(STT(ea[q, 1, :, t, :], et[q, 2], -1.0, et[q, 3], ALU.mult, ALU.subtract))

                def tok_p(n, f):
                    if f < 4:
                        j = bass.ds((n - 1) * JC, JC)
                        shape = [P, JC, NB, B]
                        c_, h_ = ((0, 0), (1, 1), (0, 1), (1, 0))[f]
                        cc = cT[:, c_, :, j].rearrange("p (o c) j -> p j o c", o=1).broadcast_to(shape)
                        hh = ph[:, h_, :, j].rearrange("p b (j o) -> p j b o", o=1).broadcast_to(shape)
                        if f == 0:
                            at_least(v, c_tokm, (n - 1) * 2)
                        ch.do(TT((pp, pt)[f % 2][:, f // 2], cc, hh, ALU.mult))
                        if f == 3:
                            ch.sync()
                    else:
                        fl = lambda t: t[:, f - 4].rearrange("p j b c -> p (j b c)")
                        ins = TT(fl(pp), fl(pp), fl(pt), ALU.subtract if f == 4 else ALU.add)
                        if f == 5:
                            ch.sync()
                            ins.then_inc(c_tokp, 1)
                        else:
                            ch.do(ins)

                def glow(n, m):
                    w, p0 = cols(n), (0 if m < SHM else SHT)
                    v.wait_ge(c_gh, n * 6 + m + 1)
                    TT(gT[p0:P, m, 1, 0:w], gf[p0:P, m % 2, 0:w], gT[p0:P, m, 0, 0:w], ALU.subtract).then_inc(c_gl, 1)

                def gprod(n, m):
                    w, p0 = cols(n), (0 if m < SHM else SHT)
                    v.wait_ge(c_sg, n * 6 + m + 1)
                    at_least(v, c_gl, n * 6 + m - 1)
                    u = BU[m % 2][:, TOK:TOK + w] if m < SHM else BU[m % 2][SHT:P, 0:w]
                    STT(gf[p0:P, m % 2, 0:w], u, SXW, sgs[p0:P, m % 2, 0:w], ALU.mult, ALU.mult).then_inc(c_gm, 1)

                def choose(n):
                    nt = tiles(n)
                    r = lambda i: rt[:, i, 0:nt, :]
                    q = lambda i: rm[:, i, 0:nt]
                    wide = lambda i: rm[:, i, 0:nt].rearrange("p (i o) -> p i o", o=1).broadcast_to([P, nt, E])
                    f = lambda ap: ap.rearrange("p i e -> p (i e)")
                    v.wait_ge(c_rt, n + 1)
                    link(TS(f(r(0)), BS[:, 0:nt * E], SXW, None, ALU.mult))
                    ch.do(nc.vector.tensor_copy(logits[:, bass.ds(rows_of(n), nt), :], r(0)))
                    for c in range(2):
                        link(RED(q(c), r(0), AX.X, ALU.max))
                        link(TT(r(1), r(0), wide(c), ALU.is_equal))
                        link(TT(r(1), r(1), rev[:, 0:nt, :], ALU.mult))
                        link(RED(q(2 + c), r(1), AX.X, ALU.max))
                        link(TT(oh[:, c, 0:nt, :], r(1), wide(2 + c), ALU.is_equal))
                        if c == 0:
                            link(STT(f(r(0)), f(oh[:, 0, 0:nt, :]), -3e38, f(r(0)), ALU.mult, ALU.add))
                    ch.do(nc.vector.tensor_copy(top_l[:, bass.ds(rows_of(n), nt), :],
                                                rm[:, 0:2, 0:nt].rearrange("p c i -> p i c")))
                    if nt == 1:
                        link(TS(oh[:, :, 0, :], oh[:, :, 0, :], mask0[:, 0:1], None, ALU.mult))
                    TT(m16[:, 0:nt, :], oh[:, 0, 0:nt, :], oh[:, 1, 0:nt, :], ALU.add).then_inc(c_m, 1)

                def place(n):
                    nt = tiles(n)
                    v.wait_ge(c_rk, n + 1)
                    at_least(v, c_sca, n * 64)
                    for i in range(nt):
                        link(TT(rt[:, 2, i, :], BS[:, 256 + i * E:256 + (i + 1) * E], run[:], ALU.add))
                        link(TT(run[:], BS[:, 288 + i * E:288 + (i + 1) * E], run[:], ALU.add))
                    for c in range(2):
                        link(TT(rt[:, 3, 0:nt, :], oh[:, c, 0:nt, :], rt[:, 2, 0:nt, :], ALU.mult))
                        link(RED(rm[:, 4 + c, 0:nt], rt[:, 3, 0:nt, :], AX.X, ALU.add))
                    both = rm[:, 4:6, 0:nt].rearrange("p c i -> p i c")
                    dst = slots[:, bass.ds(rows_of(n), nt), :]
                    if nt == 1:
                        link(TT(rm[:, 7, :], rm[:, 4:6, 0], dump_s[:], ALU.add))
                        ch.do(nc.vector.tensor_copy(slots[:, 0, :], rm[:, 4:6, 0]))
                        nc.vector.tensor_copy(sl[:, 0, :], rm[:, 7, :]).then_inc(c_sl, 1)
                    else:
                        ch.do(nc.vector.tensor_copy(dst, both))
                        nc.vector.tensor_copy(sl[:], both).then_inc(c_sl, 1)

                def scan(n):
                    w = cols(n)
                    nb = w // TC
                    v.wait_ge(c_th, n + 1)
                    ch.do(TS(om[:, 0:w], th[:, 0:w], -0.5, 0.5, ALU.mult, ALU.add))
                    ch.do(TS(al[:, 0:w], th[:, 0:w], 0.5, 0.5, ALU.mult, ALU.add))
                    link(TS(bb[:, 0:w], BB[:, 0:w], SXW, cb[:, 1:2], ALU.mult, ALU.add))
                    link(TT(bb[:, 0:w], bb[:, 0:w], al[:, 0:w], ALU.mult))
                    first = lambda t: t[:, 0:w].rearrange("p (c t) -> p c t", t=TC)[:, :, 0]
                    link(TT(fix[:, 0:nb], first(om), carry[:, 0:nb], ALU.mult))
                    link(TT(first(bb), first(bb), fix[:, 0:nb], ALU.add))
                    link(nc.vector.memset(first(om), 0.0))
                    link(nc.vector.tensor_tensor_scan(al[:, 0:w], om[:, 0:w], bb[:, 0:w], 0.0, ALU.mult, ALU.add))
                    if nb < B:
                        link(nc.vector.tensor_copy(carry[:], al[:, 0:1].broadcast_to([P, B])))
                    else:
                        link(nc.vector.tensor_copy(carry[:], al[:, 0:w].rearrange("p (c t) -> p c t", t=TC)[:, :, TC - 1]))
                    at_least(v, c_yl, n)
                    STT(hsc[:, 0:w], al[:, 0:w], SY, tc[:, 0:w], ALU.mult, ALU.mult).then_inc(c_yf, 1)

                def normed(n, i):
                    nt = tiles(n)
                    v.wait_ge(c_pw3, n * 2 + (i + 1) * 2 // nt)
                    if has(n + 1):
                        v.wait_ge(c_lo2, n + 2)
                    TS(xf[:, i, :], h2[:, i, :], mv[:, 1, i, 0:1], sc[:, 6, i:i + 1], ALU.subtract,
                       ALU.mult).then_inc(c_xf3, 2 // nt)

                def rows_lo(n, i):
                    nt = tiles(n)
                    v.wait_ge(c_hi3, n * 2 + (i + 1) * 2 // nt)
                    TT(x3r[:, i, 1, :], xf[:, i, :], x3r[:, i, 0, :], ALU.subtract).then_inc(c_lo3, 2 // nt)

                def body(k):
                    def stats2(n):
                        nt = tiles(n)
                        v.wait_ge(c_hx, (n + 1) * 16)
                        for i in range(nt):
                            ch.do(nc.vector.bn_stats(stat[:, 0, i, :], hx[:, i, :]))
                        ch.sync()
                        apart(v, c_sep)
                        if nt == 1:
                            ch.do(nc.vector.memset(mv[:], 1.0))
                            ch.sync()
                        for i in range(nt):
                            last = nc.vector.bn_aggr(mv[:, 0, i, :], stat[:, 0, i, :])
                        last.then_inc(c_st2, 1)

                    if has(k - 1):
                        gprod(k - 1, 0)
                    if has(k):
                        w = cols(k)
                        v.wait_ge(c_yh, k + 1)
                        TT(yT[:, 1, 0:w], hsc[:, 0:w], yT[:, 0, 0:w], ALU.subtract).then_inc(c_yl, 1)
                    if has(k - 1):
                        gprod(k - 1, 1)
                        choose(k - 1)
                    if htok(k + 2):
                        tok_p(k + 2, 0)
                    for m in range(5):
                        if has(k - 1):
                            glow(k - 1, m)
                            if m < 4:
                                gprod(k - 1, m + 2)
                            if m == 1:
                                place(k - 1)
                        if m == 0 and has(k + 1):
                            stats2(k + 1)
                        if m in (2, 3) and htok(k + 2):
                            tok_p(k + 2, m - 1)
                    if has(k - 1):
                        glow(k - 1, 5)
                    if has(k + 1):
                        n, nt = k + 1, tiles(k + 1)
                        v.wait_ge(c_pw2, n + 1)
                        at_least(v, c_hi3, 2 * n - 2)
                        for i in range(nt):
                            last = TS(xf[:, i, :], hx[:, i, :], mv[:, 0, i, 0:1], sc[:, 3, i:i + 1], ALU.subtract, ALU.mult)
                        last.then_inc(c_xf2, 1)
                        if htok(k + 2):
                            tok_p(k + 2, 3)
                        v.wait_ge(c_hi2, n + 1)
                        TT(x2r[:, 0:nt, 1, :], xf[:, 0:nt, :], x2r[:, 0:nt, 0, :], ALU.subtract).then_inc(c_lo2, 1)
                    for i in range(2):
                        if has(k - 1) and i < tiles(k - 1):
                            n, nt = k - 1, tiles(k - 1)
                            v.wait_ge(c_dn, n * 2 + (i + 1) * 2 // nt)
                            at_least(v, c_ro, n * 16)
                            STT(r_o[:, i, :], BD[:], 1.0 / SW, h2[:, i, :], ALU.mult, ALU.add).then_inc(c_dev, 2 // nt)
                        if htok(k + 2) and i == 0:
                            tok_p(k + 2, 4)
                        if has(k) and i < tiles(k):
                            n, nt = k, tiles(k)
                            v.wait_ge(c_out, n * 2 + (i + 1) * 2 // nt)
                            v.wait_ge(c_prom, n + 1)
                            if has(k - 1):
                                v.wait_ge(c_dev, (k - 1) * 2 + (2 if tiles(k - 1) == 1 else i + 1))
                            link(STT(h2[:, i, :], BS[:], ir[:, i:i + 1], hc[:, i, :], ALU.mult, ALU.add))
                            STT(h2[:, i, :], BY[:], 1.0 / (SW * SY), h2[:, i, :], ALU.mult, ALU.add).then_inc(c_oev, 2 // nt)
                            v.wait_ge(c_oev, n * 2 + (i + 1) * 2 // nt)
                            link(nc.vector.bn_stats(stat[:, 1, i, :], h2[:, i, :]))
                            apart(v, c_sep)
                            nc.vector.bn_aggr(mv[:, 1, i, :], stat[:, 1, i, :]).then_inc(c_st3, 2 // nt)
                        if htok(k + 2) and i == 0:
                            tok_p(k + 2, 5)
                        if htok(k + 3) and i == 1:
                            tok_e(k + 3, 0)
                        if has(k) and i < tiles(k):
                            normed(k, i)
                        if htok(k + 3) and i == 1:
                            tok_e(k + 3, 1)
                        if has(k) and i < tiles(k):
                            rows_lo(k, i)
                    if htok(k + 3):
                        for f in range(2, 5):
                            tok_e(k + 3, f)
                    if has(k + 1):
                        scan(k + 1)

                ch.do(nc.vector.memset(carry[:], 0.0))
                link(nc.vector.memset(ea[:].rearrange("p f j t a -> p (f j t a)"), 0.0))
                nc.vector.memset(hdn[HK[2]:P, 2, :, :], 0.0).then_inc(c_cst, 1)
                nc.vector.memset(m16[:], 0.0).then_inc(c_cst, 1)
                v.wait_ge(c_cst, 2)
                for f in range(5):
                    tok_e(1, f)
                iterate(v, body, ch, PER_DVE)
                v.wait_ge(c_sl, NCH + 1)
                TS(zi[:], run[:], pcol[:, 0:1], None, ALU.add).then_inc(c_cst, 1)

        phase1.close()

        wts = keep("wts", [P, TILES, 2], F32)
        tbl = keep("tbl", [P, 3, NSLOT], I32)
        with ExitStack() as ph2:
            t2 = sb_in(ph2)
            wexp = t2("wexp", [P, 2 * E, UW], F16)
            xr = [t2(f"xr{b}", [P, 2, D], F16) for b in range(2)]
            yo = [t2(f"yo{b}", [P, D], F32) for b in range(2)]
            xT = t2("xT", [P, 2, KD, P], F16)
            sg = t2("sg", [P, H], F32)
            gx = t2("gx", [P, H], F32)
            gh = t2("gh", [P, 2, H], F16)
            gT2 = [t2(f"gT2{b}", [P, 2, KH, P], F16) for b in range(2)]
            io1 = t2("io1", [P, TILES], I32)
            io2 = t2("io2", [P, NSLOT], I32)
            jf = t2("jf", [P, TILES], F32)
            jn = t2("jn", [P, NSLOT], F32)
            cmp1 = t2("cmp1", [P, E, TILES], F32)
            cmp2 = t2("cmp2", [P, NSLOT, E], F32)
            cmp3 = t2("cmp3", [P, NSLOT, E], F32)
            used = t2("used", [P, 3, E], F32)
            jt = t2("jt", [P, 6, NSLOT], F32)
            lx = t2("lx", [P, TILES, E + 1], F32)
            lt = t2("lt", [P, TILES], F32)
            rg = t2("rg", [P, TILES, 2], F32)
            rh = t2("rh", [P, TILES, 2], F32)

            XB, GB, UB, TB, DB = psum[0], psum[1], psum[2], psum[3], psum[4]

            d_w = sem("d_w")
            d_tb = sem("d_tb")
            d_io = sem("d_io")
            d_lx = sem("d_lx")
            d_xl = [sem("d_xl0"), sem("d_xl1")]
            d_ys = [sem("d_ys0"), sem("d_ys1")]
            d_xt = sem("d_xt")
            d_xe = sem("d_xe")
            d_gu = sem("d_gu")
            d_sg = sem("d_sg")
            d_gf = sem("d_gf")
            d_gh = sem("d_gh")
            d_gl = sem("d_gl")
            d_gt = sem("d_gt")
            d_ge = sem("d_ge")
            d_dn = sem("d_dn")
            d_ye = sem("d_ye")
            d_sep = sem("d_sep")
            d_v = sem("d_v")

            def over_tiles(eng, body):
                for b in range(2):
                    body(b, b)
                with eng.Fori(1, NSLOT // 2 - 1) as ii:
                    for b in range(2):
                        body(ii * 2 + b, b)
                for b in range(2):
                    body(NSLOT - 2 + b, b)

            at_end = lambda i: isinstance(i, int) and i >= NSLOT
            halfcount = lambda i, b: (i - b) * 8 + 16

            block = ph2.enter_context(nc.Block())

            @block.gpsimd
            def _(gp):
                nc.gpsimd.iota(io1[:], pattern=[[P, TILES]], base=0, channel_multiplier=0).then_inc(d_io, 1)
                nc.gpsimd.iota(io2[:], pattern=[[1, NSLOT]], base=0, channel_multiplier=0).then_inc(d_io, 1)
                for e in range(E):
                    at_least(gp, d_w, 16 * e)
                    gp.dma_start(wexp[:, 2 * e:2 * e + 2, :], w16_d[2 * e:2 * e + 2].rearrange("u p n -> p u n")).then_inc(d_w, 16)
                gp.wait_ge(d_w, 16 * E)

            @block.sync
            def _(sp):
                def load(i, b):
                    row = sp.value_load(tbl[0:1, 1, bass.ds(i, 1)], min_val=0, max_val=NR - P)
                    sp.dma_start(xr[b][:].rearrange("p h d -> p (h d)"), xs_d[bass.ds(row, P), :]).then_inc(d_xl[b], 16)

                def store(i, b):
                    sp.wait_ge(d_ye, i + 1)
                    sp.dma_start(ys_d[bass.ds(i * P, P), :], yo[b][:]).then_inc(d_ys[b], 16)

                def body(i, b):
                    if not at_end(i + 2):
                        sp.wait_ge(d_xt, i + 1)
                        load(i + 2, b)
                    if not isinstance(i, int) or i > 1:
                        store(i - 2, b)

                sp.wait_ge(d_tb, 1)
                for b in range(2):
                    load(b, b)
                over_tiles(sp, body)
                for b in range(2):
                    store(NSLOT - 2 + b, b)
                for b in range(2):
                    sp.wait_ge(d_ys[b], 16 * (NSLOT // 2))

            @block.tensor
            def _(pe):
                MM = nc.tensor.matmul
                X16, T16 = XB[:].bitcast(F16), TB[:].bitcast(F16)

                def rows_T(i, b):
                    pe.wait_ge(d_xl[b], halfcount(i, b))
                    at_least(pe, d_xe, i)
                    for h in range(2):
                        for c in range(KD):
                            last = nc.tensor.transpose(X16[:, (h * KD + c) * P:(h * KD + c + 1) * P],
                                                       xr[b][:, h, c * P:(c + 1) * P], ident16[:])
                    last.then_inc(d_xt, 1)

                def gate_up(i, unit):
                    pe.wait_ge(d_xe, i + 1)
                    at_least(pe, d_gf, i)
                    for c in range(KD):
                        for a, w in ((0, 0), (0, 1), (1, 0)):
                            u, o = bass.ds(unit + c // 2, 1), (c % 2 * 2 + w) * 2 * H
                            s_, e_ = (c == 0 and a + w == 0), (c == KD - 1 and a == 1)
                            MM(GB[:, 0:H], xT[:, a, c, :], wexp[:, u, o:o + H], start=s_, stop=e_)
                            last = MM(UB[:, 0:H], xT[:, a, c, :], wexp[:, u, o + H:o + 2 * H], start=s_, stop=e_)
                    last.then_inc(d_gu, 1)

                def down(i, b, unit):
                    pe.wait_ge(d_ge, i + 1)
                    at_least(pe, d_ye, i)
                    for c in range(KH):
                        for a, w in ((0, 0), (0, 1), (1, 0)):
                            o = UG + (c * 2 + w) * (D // 2)
                            last = MM(DB[:], gT2[b][0:HK[c], a, c, :], wexp[0:HK[c], bass.ds(unit, 2), o:o + D // 2],
                                      start=(c == 0 and a + w == 0), stop=(c == KH - 1 and a == 1))
                    last.then_inc(d_dn, 1)

                def prod_T(i):
                    pe.wait_ge(d_gh, i + 1)
                    pe.wait_ge(d_gl, i + 1)
                    at_least(pe, d_ge, i)
                    for h in range(2):
                        for c in range(KH):
                            last = nc.tensor.transpose(T16[0:HK[c], (h * KH + c) * P:(h * KH + c + 1) * P],
                                                       gh[:, h, c * P:c * P + HK[c]], ident16[:])
                    last.then_inc(d_gt, 1)

                def unit_of(i):
                    apart(pe, d_sep)
                    return pe.value_load(tbl[0:1, 0, bass.ds(i, 1)], min_val=0, max_val=2 * (E - 1))

                def body(i, b):
                    unit = unit_of(i)
                    before = unit_of(i - 2) if not isinstance(i, int) or i > 1 else None
                    pe.wait_ge(d_w, unit * 8 + 16)
                    gate_up(i, unit)
                    if not isinstance(i, int) or i > 0:
                        prod_T(i - 1)
                    if not at_end(i + 1):
                        rows_T(i + 1, 1 - b)
                    if not isinstance(i, int) or i > 1:
                        down(i - 2, b, before)

                pe.wait_ge(d_tb, 1)
                rows_T(0, 0)
                over_tiles(pe, body)
                prod_T(NSLOT - 1)
                for b in range(2):
                    down(NSLOT - 2 + b, b, unit_of(NSLOT - 2 + b))

            @block.scalar
            def _(act):
                A = nc.scalar.activation

                def rows_out(i):
                    act.wait_ge(d_xt, i + 1)
                    at_least(act, d_gu, i)
                    A(xT[:].rearrange("p h k t -> p (h k t)"), XB[:].bitcast(F16), ACT.Copy).then_inc(d_xe, 1)

                def body(i, b):
                    act.wait_ge(d_gu, i + 1)
                    A(sg[:], GB[:, 0:H], ACT.Silu, scale=SXW).then_inc(d_sg, 1)
                    if not at_end(i + 1):
                        rows_out(i + 1)
                    act.wait_ge(d_gf, i + 1)
                    at_least(act, d_gt, i)
                    A(gh[:, 0, :], gx[:], ACT.Copy).then_inc(d_gh, 1)

                act.wait_ge(d_lx, 1)
                A(lx[:], lx[:], ACT.Exp).then_inc(d_lx, 1)
                rows_out(0)
                over_tiles(act, body)

            @block.vector
            def _(v):
                ch = Chain(v, d_v)
                link = ch.link
                TT, TS, STT = nc.vector.tensor_tensor, nc.vector.tensor_scalar, nc.vector.scalar_tensor_tensor
                RED = nc.vector.tensor_reduce
                v.wait_ge(d_io, 2)
                ch.do(nc.vector.tensor_copy(jf[:], io1[:]))
                link(nc.vector.tensor_copy(jn[:], io2[:]))
                link(TS(used[:, 0, :], rev[:, 0, :], float(CAP), -float(CAP * E), ALU.mult, ALU.add))
                link(TT(used[:, 0, :], run[:], used[:, 0, :], ALU.add))
                e_by = lambda ap, n: ap.rearrange("p (e o) -> p e o", o=1).broadcast_to([P, E, n])
                link(TT(cmp1[:], e_by(used[:, 0, :], TILES), jf[:].rearrange("p (o j) -> p o j", o=1).broadcast_to([P, E, TILES]),
                        ALU.is_gt))
                link(RED(used[:, 1, :], cmp1[:], AX.X, ALU.add))
                link(nc.vector.memset(used[:, 0, :], 1.0))
                link(nc.vector.tensor_tensor_scan(used[:, 2, :], used[:, 0, :], used[:, 1, :], 0.0, ALU.mult, ALU.add))
                by_j = lambda ap: ap.rearrange("p (o e) -> p o e", o=1).broadcast_to([P, NSLOT, E])
                link(TT(cmp2[:], jn[:].rearrange("p (j o) -> p j o", o=1).broadcast_to([P, NSLOT, E]), by_j(used[:, 2, :]), ALU.is_ge))
                link(RED(jt[:, 0, :], cmp2[:], AX.X, ALU.add))
                link(TT(cmp3[:], cmp2[:], by_j(used[:, 1, :]), ALU.mult))
                link(RED(jt[:, 1, :], cmp3[:], AX.X, ALU.add))
                link(TS(jt[:, 2, :], jt[:, 0, :], float(E), None, ALU.is_lt))
                link(TT(jt[:, 3, :], jn[:], jt[:, 1, :], ALU.subtract))
                link(TS(jt[:, 3, :], jt[:, 3, :], float(P), None, ALU.mult))
                link(STT(jt[:, 3, :], jt[:, 0, :], float(CAP), jt[:, 3, :], ALU.mult, ALU.add))
                link(TT(jt[:, 0, :], jt[:, 0, :], jt[:, 2, :], ALU.mult))
                link(TS(tbl[:, 0, :], jt[:, 0, :], 2.0, None, ALU.mult))
                link(TS(tbl[:, 2, :], jt[:, 0, :], 16.0, 16.0, ALU.mult, ALU.add))
                link(TS(jt[:, 4, :], jt[:, 3, :], -float(ZERO), None, ALU.add))
                link(TT(jt[:, 4, :], jt[:, 4, :], jt[:, 2, :], ALU.mult))
                TS(tbl[:, 1, :], jt[:, 4, :], float(ZERO), None, ALU.add).then_inc(d_tb, 1)
                link(TS(used[:, 0, :], used[:, 1, :], float(P), -float(CAP), ALU.mult, ALU.add))
                link(nc.vector.tensor_copy(rg[:], slots[:]))
                for e in range(E - 1):
                    link(TS(rh[:], slots[:], float((e + 1) * CAP), used[:, 0, e:e + 1], ALU.is_ge, ALU.mult))
                    link(TT(rg[:], rg[:], rh[:], ALU.add))
                link(nc.vector.tensor_copy(rows_y[:, 0:TILES, :], rg[:]))
                wide = lambda ap: ap.broadcast_to([P, TILES, E])
                link(TT(lx[:, :, 0:E], logits[:], wide(top_l[:, :, 0:1]), ALU.subtract))
                TT(lx[:, :, E], top_l[:, :, 1], top_l[:, :, 0], ALU.subtract).then_inc(d_lx, 1)
                v.wait_ge(d_lx, 2)
                link(RED(lt[:], lx[:, :, 0:E], AX.X, ALU.add))
                link(nc.vector.reciprocal(wts[:, :, 0], lt[:]))
                link(TT(wts[:, :, 1], wts[:, :, 0], lx[:, :, E], ALU.mult))

                def out_of(i, b):
                    v.wait_ge(d_dn, i + 1)
                    at_least(v, d_ys[b], halfcount(i, b) - 16)
                    TS(yo[b][:], DB[:], 1.0 / SW, None, ALU.mult).then_inc(d_ye, 1)

                def body(i, b):
                    v.wait_ge(d_sg, i + 1)
                    at_least(v, d_gl, i)
                    STT(gx[:], UB[:, 0:H], SXW, sg[:], ALU.mult, ALU.mult).then_inc(d_gf, 1)
                    if not isinstance(i, int) or i > 0:
                        prod_out(i - 1, 1 - b)
                    v.wait_ge(d_gh, i + 1)
                    TT(gh[:, 1, :], gx[:], gh[:, 0, :], ALU.subtract).then_inc(d_gl, 1)
                    if not isinstance(i, int) or i > 1:
                        out_of(i - 2, b)

                def prod_out(i, b):
                    v.wait_ge(d_gt, i + 1)
                    at_least(v, d_dn, i - 1)
                    T16 = TB[:].bitcast(F16)
                    tt = lambda c0, c1: T16[:, 0:2 * KH * P].rearrange("p (h c t) -> p h c t", h=2, c=KH)[:, :, c0:c1, :]
                    nc.vector.tensor_copy(gT2[b][:, :, 0:KH - 1, :], tt(0, KH - 1))
                    nc.vector.tensor_copy(gT2[b][0:HK[-1], :, KH - 1:KH, :], tt(KH - 1, KH)[0:HK[-1]]).then_inc(d_ge, 1)

                over_tiles(v, body)
                prod_out(NSLOT - 1, 1)
                for b in range(2):
                    out_of(NSLOT - 2 + b, b)

        with ExitStack() as ph3:
            t3 = sb_in(ph3)
            idx = t3("idx", [P, NBUF, 2], I32)
            rr = t3("rr", [P, NBUF, D], F32)
            y1 = t3("y1", [P, NBUF, 2, D], F32)
            e_r = [sem(f"e_r{b}") for b in range(NBUF)]
            e_y = [sem(f"e_y{b}") for b in range(NBUF)]
            e_o = [sem(f"e_o{b}") for b in range(NBUF)]
            e_f = sem("e_f")
            e_i = [sem(f"e_i{b}") for b in range(NBUF)]
            e_sep = sem("e_sep")
            e_m = sem("e_m")
            block = ph3.enter_context(nc.Block())
            assert (TILES - 1) % NBUF == 0
            GR = (TILES - 1) // NBUF

            def before(g, b):
                return g + (1 if b == 0 else 0)

            def run_groups(eng, body):
                body(0, 0, 0, 0)
                for b in range(NBUF):
                    body(b + 1, before(0, b), b, 0)
                with eng.Fori(1, GR) as g:
                    for b in range(NBUF):
                        body(g * NBUF + (b + 1), before(g, b), b, g)

            @block.sync
            def _(sp):
                def body(tile, n, b, g):
                    at_least(sp, e_o[b], n * 16)
                    sp.dma_start(rr[:, b, :], rs_d[bass.ds(tile * P, P), :]).then_inc(e_r[b], 16)
                run_groups(sp, body)

            @block.gpsimd
            def _(gp):
                def body(tile, n, b, g):
                    at_least(gp, e_o[b], n * 16)
                    gp.wait_ge(e_i[b], n + 1)
                    apart(gp, e_sep)
                    for c in range(2):
                        nc.gpsimd.indirect_dma_start(out=y1[:, b, c, :], out_offset=None, in_=ys_d,
                                                     in_offset=bass.IndirectOffsetOnAxis(ap=idx[:, b, c:c + 1], axis=0)).then_inc(e_y[b], 16)
                run_groups(gp, body)

            @block.vector
            def _(v):
                STT = nc.vector.scalar_tensor_tensor

                def body(tile, n, b, g):
                    v.wait_ge(e_r[b], n * 16 + 16)
                    v.wait_ge(e_y[b], n * 32 + 32)
                    after = 1 if isinstance(tile, int) and tile == 0 else tile + NBUF
                    nc.vector.tensor_copy(idx[:, b:b + 1, :], rows_y[:, bass.ds(after, 1), :]).then_inc(e_i[b], 1)
                    wv = lambda c: wts[:, bass.ds(tile, 1), c]
                    STT(rr[:, b, :], y1[:, b, 0, :], wv(0), rr[:, b, :], ALU.mult, ALU.add).then_inc(e_m, 1)
                    v.wait_ge(e_m, tile + 1)
                    STT(rr[:, b, :], y1[:, b, 1, :], wv(1), rr[:, b, :], ALU.mult, ALU.add).then_inc(e_f, 1)
                nc.vector.tensor_copy(idx[:, 0, :], rows_y[:, 0, :]).then_inc(e_i[0], 1)
                for b in range(1, NBUF):
                    nc.vector.tensor_copy(idx[:, b, :], rows_y[:, 1 + b, :]).then_inc(e_i[b], 1)
                run_groups(v, body)

            @block.scalar
            def _(act):
                def body(tile, n, b, g):
                    act.wait_ge(e_f, tile + 1)
                    if isinstance(tile, int) and tile == 0:
                        act.dma_start(out[:, 0:1, :].rearrange("(o c) t d -> o c (t d)", o=1),
                                      rr[0:1, b, :].rearrange("p (o d) -> p o d", o=1).broadcast_to([1, B, D])).then_inc(e_o[b], 16)
                        return
                    c0 = (b % 2) * (B // 2)
                    t0_ = g * (2 * TC) + (1 + (b // 2) * TC)
                    act.dma_start(out[c0:c0 + B // 2, bass.ds(t0_, TC), :], rr[:, b, :]).then_inc(e_o[b], 16)
                run_groups(act, body)
                for b in range(NBUF):
                    act.wait_ge(e_o[b], 16 * (GR + (b == 0)))


_INS = ["x", "cls_tok", "L0_tok_log_dt", "L0_tok_B_ri", "L0_tok_inv_A_real", "L0_tok_A_imag", "L0_attn_gamma", "L0_attn_beta",
        "L0_attn_W_in", "L0_attn_b_in", "L0_attn_W_out", "L0_attn_b_out", "L0_attn_W_skip", "L0_attn_b_skip", "L0_ffn_gate_w",
        "L0_ffn_w_gate", "L0_ffn_w_up", "L0_ffn_w_down", "L0_ffn_sw_gate", "L0_ffn_sw_up", "L0_ffn_sw_down"]


def kernel(**inputs):
    import numpy as _np
    import concourse.bacc as _bacc
    from concourse import mybir as _mybir
    from concourse.bass_utils import run_bass_kernel_spmd as _run

    nc = _bacc.Bacc("TRN2", target_bir_lowering=False, num_devices=1)
    arrays, args = {}, []
    for name in _INS:
        a = _np.ascontiguousarray(inputs[name])
        arrays["in_" + name] = a
        args.append(nc.dram_tensor("in_" + name, a.shape, _mybir.dt.from_np(a.dtype), kind="ExternalInput").ap())
    out = nc.dram_tensor("out", (B, T + 1, D), F32, kind="ExternalOutput").ap()
    vit_tower(nc, *args, out)
    r = _run(nc, [arrays], core_ids=[0])
    return r.results[0]["out"]
```
